# Optimizing a Trainium2 kernel written in Bass

```python
import numpy as np
import jax
import jax.numpy as jnp

def _softmax(x, axis=-1):
    return jax.nn.softmax(x, axis=axis)

def _gelu(x):
    return jax.nn.gelu(x, approximate=True)

def _silu(x):
    return jax.nn.silu(x)

def _sigmoid(x):
    return jax.nn.sigmoid(x)

def _layernorm(x, axis=-1, eps=1e-05):
    m = jnp.mean(x, axis=axis, keepdims=True)
    v = jnp.var(x, axis=axis, keepdims=True)
    return (x - m) / jnp.sqrt(v + eps)

def _scatter_add(tgt, idx, src, axis=0):
    return tgt.at[idx].add(src)

def _segment_sum(src, seg, n):
    return jax.ops.segment_sum(src, seg, n)
kernel_name = 'mk_gnn_resnorm_d4_gnn_r32_0c81b4'

def setup_inputs(seed: int=0):
    np.random.seed(seed)
    _w = jnp.asarray

    def _rec_inputs():
        import jax
        import jax.numpy as jnp
        _gk = jax.random.key(seed)
        x = -0.000202 + 1 * jax.random.normal(jax.random.fold_in(_gk, 1), (3125, 64), jnp.float32)
        _s = jax.random.randint(jax.random.fold_in(_gk, 2), (50000,), 0, 3125, jnp.int32)
        _d = jax.random.randint(jax.random.fold_in(_gk, 3), (50000,), 0, 3125, jnp.int32)
        _loop = jnp.arange(3125, dtype=jnp.int32)
        src = jnp.concatenate([_s, _d, _loop])
        dst = jnp.concatenate([_d, _s, _loop])
        _o = jnp.argsort(dst, stable=True)
        src = src[_o]
        dst = dst[_o]
        edge_attr_16 = 0.000196303 + 1.00016 * jax.random.normal(jax.random.fold_in(_gk, 12), (103125, 16), jnp.float32)
        edge_attr_64 = -2.25437e-05 + 0.999858 * jax.random.normal(jax.random.fold_in(_gk, 13), (103125, 64), jnp.float32)
        return (x, src, dst, edge_attr_16, edge_attr_64)
    x, src, dst, edge_attr_16, edge_attr_64 = _rec_inputs()

    def _L0_gnn_setup():
        import jax, jax.numpy as jnp
        import numpy as np
        N, E = (3125, 50000)
        IN_DIM, OUT_DIM, EDGE_DIM, H = (64, 64, 16, 4)
        HD = OUT_DIM // H
        NEG_SLOPE = 0.2
        EPS_SOFTMAX = 1e-08
        EPS_LN = 1e-05
        key = jax.random.key(seed)
        ks = jax.random.split(key, 8)
        return {'x': jax.random.normal(ks[0], (N, IN_DIM), jnp.float32), 'edge_index': jax.random.randint(ks[1], (2, E), 0, N, jnp.int64 if jax.config.jax_enable_x64 else jnp.int32), 'edge_attr': jax.random.normal(ks[2], (E, EDGE_DIM), jnp.float32), 'W_node': jax.random.normal(ks[3], (IN_DIM, OUT_DIM), jnp.float32) / np.sqrt(IN_DIM), 'W_edge': jax.random.normal(ks[4], (EDGE_DIM, H), jnp.float32) / np.sqrt(EDGE_DIM), 'attn_src': jax.random.normal(ks[5], (H, HD), jnp.float32), 'attn_dst': jax.random.normal(ks[6], (H, HD), jnp.float32), 'ln_gamma': jnp.ones((OUT_DIM,), jnp.float32), 'ln_beta': jnp.zeros((OUT_DIM,), jnp.float32)}
    _L0_gnn_all = _L0_gnn_setup()
    _L0_gnn_in = {k: v for k, v in _L0_gnn_all.items() if k in ('W_node', 'W_edge', 'attn_src', 'attn_dst', 'ln_gamma', 'ln_beta')}
    del _L0_gnn_all

    def _L1_gnn_setup():
        import jax, jax.numpy as jnp
        import numpy as np
        N_NODES = 3125
        N_EDGES = 31250
        D_FEAT = 64
        THETA = (1.0, 0.8, 0.5, 0.3)
        key = jax.random.key(seed)
        k1, k2, k3 = jax.random.split(key, 3)
        feat = jax.random.normal(k1, (N_NODES, D_FEAT), dtype=jnp.float32)
        src = jax.random.randint(k2, (N_EDGES,), 0, N_NODES, dtype=jnp.int32)
        dst = jax.random.randint(k3, (N_EDGES,), 0, N_NODES, dtype=jnp.int32)
        return {'feat': feat, 'src': src, 'dst': dst}
    _L1_gnn_all = _L1_gnn_setup()
    _L1_gnn_in = {k: v for k, v in _L1_gnn_all.items() if k in ()}
    del _L1_gnn_all

    def _L2_gnn_setup():
        import jax, jax.numpy as jnp
        import numpy as np
        N_NODES = 3125
        N_EDGES = 31250
        D_NODE = 64
        D_EDGE = 64
        NUM_LAYERS = 3
        EPS = 1e-12

        def _l2norm(h):
            n = jnp.sqrt(jnp.sum(h * h, axis=-1, keepdims=True))
            return h / jnp.maximum(n, EPS)
        key = jax.random.key(seed)
        ks = jax.random.split(key, 10)
        s = 0.05
        inp = {'x': jax.random.normal(ks[0], (N_NODES, D_NODE), jnp.float32), 'edge_attr': jax.random.normal(ks[1], (N_EDGES, D_EDGE), jnp.float32), 'edge_index': jax.random.randint(ks[2], (2, N_EDGES), 0, N_NODES, jnp.int32), 'msg_W': jax.random.normal(ks[3], (NUM_LAYERS, D_NODE + D_EDGE, D_NODE), jnp.float32) * s, 'msg_b': jnp.zeros((NUM_LAYERS, D_NODE), jnp.float32), 'agg_W': jax.random.normal(ks[4], (NUM_LAYERS, D_NODE + D_NODE, D_NODE), jnp.float32) * s, 'agg_b': jnp.zeros((NUM_LAYERS, D_NODE), jnp.float32), 'edge_W': jax.random.normal(ks[5], (NUM_LAYERS - 1, 2 * D_NODE + D_EDGE, D_EDGE), jnp.float32) * s, 'edge_b': jnp.zeros((NUM_LAYERS - 1, D_EDGE), jnp.float32)}
        return inp
    _L2_gnn_all = _L2_gnn_setup()
    _L2_gnn_in = {k: v for k, v in _L2_gnn_all.items() if k in ('msg_W', 'msg_b', 'agg_W', 'agg_b', 'edge_W', 'edge_b')}
    del _L2_gnn_all

    def _L3_gnn_setup():
        import jax, jax.numpy as jnp
        import numpy as np
        NUM_NODES = 50000
        EMBED_DIM = 64
        NUM_EDGES = 1250000
        NUM_LAYERS = 3
        key = jax.random.key(seed)
        k1, k2 = jax.random.split(key)
        edge_index = jax.random.randint(k1, (2, NUM_EDGES), 0, NUM_NODES, dtype=jnp.int64) if jax.config.read('jax_enable_x64') else jax.random.randint(k1, (2, NUM_EDGES), 0, NUM_NODES, dtype=jnp.int32)
        embedding_weight = jax.random.normal(k2, (NUM_NODES, EMBED_DIM), dtype=jnp.float32)
        return {'edge_index': edge_index, 'embedding_weight': embedding_weight}
    _L3_gnn_all = _L3_gnn_setup()
    _L3_gnn_in = {k: v for k, v in _L3_gnn_all.items() if k in ()}
    del _L3_gnn_all
    return {'x': x, 'src': src, 'dst': dst, 'edge_attr_16': edge_attr_16, 'edge_attr_64': edge_attr_64, 'L0_gnn_W_node': _L0_gnn_in['W_node'], 'L0_gnn_W_edge': _L0_gnn_in['W_edge'], 'L0_gnn_attn_src': _L0_gnn_in['attn_src'], 'L0_gnn_attn_dst': _L0_gnn_in['attn_dst'], 'L0_gnn_ln_gamma': _L0_gnn_in['ln_gamma'], 'L0_gnn_ln_beta': _L0_gnn_in['ln_beta'], 'L2_gnn_msg_W': _L2_gnn_in['msg_W'], 'L2_gnn_msg_b': _L2_gnn_in['msg_b'], 'L2_gnn_agg_W': _L2_gnn_in['agg_W'], 'L2_gnn_agg_b': _L2_gnn_in['agg_b'], 'L2_gnn_edge_W': _L2_gnn_in['edge_W'], 'L2_gnn_edge_b': _L2_gnn_in['edge_b']}

def reference(x, src, dst, edge_attr_16, edge_attr_64, L0_gnn_W_node, L0_gnn_W_edge, L0_gnn_attn_src, L0_gnn_attn_dst, L0_gnn_ln_gamma, L0_gnn_ln_beta, L2_gnn_msg_W, L2_gnn_msg_b, L2_gnn_agg_W, L2_gnn_agg_b, L2_gnn_edge_W, L2_gnn_edge_b):
    import jax
    import jax.numpy as jnp

    def _L0_gnn_ref(x, edge_index, edge_attr, W_node, W_edge, attn_src, attn_dst, ln_gamma, ln_beta):
        import jax, jax.numpy as jnp
        import numpy as np
        N, E = (3125, 50000)
        IN_DIM, OUT_DIM, EDGE_DIM, H = (64, 64, 16, 4)
        HD = OUT_DIM // H
        NEG_SLOPE = 0.2
        EPS_SOFTMAX = 1e-08
        EPS_LN = 1e-05
        n = x.shape[0]
        src, dst = (edge_index[0], edge_index[1])
        h = (x @ W_node).reshape(n, H, HD)
        a_src_node = jnp.einsum('nhd,hd->nh', h, attn_src)
        a_dst_node = jnp.einsum('nhd,hd->nh', h, attn_dst)
        e_score = edge_attr @ W_edge
        attn = a_src_node[src] + a_dst_node[dst] + e_score
        attn = jnp.where(attn >= 0, attn, NEG_SLOPE * attn)
        attn_max = jnp.zeros((n, H), attn.dtype).at[dst].max(attn)
        attn = jnp.exp(attn - attn_max[dst])
        attn_sum = jnp.zeros((n, H), attn.dtype).at[dst].add(attn)
        attn = attn / (attn_sum[dst] + EPS_SOFTMAX)
        msg = h[src] * attn[:, :, None]
        out = jnp.zeros((n, H, HD), h.dtype).at[dst].add(msg).reshape(n, OUT_DIM)
        y = out + h.reshape(n, OUT_DIM)
        mu = jnp.mean(y, axis=-1, keepdims=True)
        var = jnp.mean((y - mu) ** 2, axis=-1, keepdims=True)
        return (y - mu) * jax.lax.rsqrt(var + EPS_LN) * ln_gamma + ln_beta

    def _L1_gnn_ref(feat, src, dst):
        import jax, jax.numpy as jnp
        import numpy as np
        N_NODES = 3125
        N_EDGES = 31250
        D_FEAT = 64
        THETA = (1.0, 0.8, 0.5, 0.3)
        n = feat.shape[0]
        deg = jax.ops.segment_sum(jnp.ones_like(dst, dtype=feat.dtype), dst, num_segments=n)
        d_invsqrt = jnp.power(jnp.clip(deg, 1.0, None), -0.5)[:, None]
        h = THETA[0] * feat
        for k in range(1, len(THETA)):
            msg = (feat * d_invsqrt)[src]
            agg = jax.ops.segment_sum(msg, dst, num_segments=n)
            feat = feat - agg * d_invsqrt
            h = h + THETA[k] * feat
        return h

    def _L2_gnn_ref(x, edge_attr, edge_index, msg_W, msg_b, agg_W, agg_b, edge_W, edge_b):
        import jax, jax.numpy as jnp
        import numpy as np
        N_NODES = 3125
        N_EDGES = 31250
        D_NODE = 64
        D_EDGE = 64
        NUM_LAYERS = 3
        EPS = 1e-12

        def _l2norm(h):
            n = jnp.sqrt(jnp.sum(h * h, axis=-1, keepdims=True))
            return h / jnp.maximum(n, EPS)
        src = edge_index[0]
        dst = edge_index[1]
        n = x.shape[0]
        num_layers = msg_W.shape[0]
        cnt = jax.ops.segment_sum(jnp.ones((src.shape[0],), x.dtype), dst, num_segments=n)
        inv_cnt = (1.0 / jnp.maximum(cnt, 1.0))[:, None]
        for l in range(num_layers):
            m = jnp.concatenate([x[src], edge_attr], axis=-1) @ msg_W[l] + msg_b[l]
            m = jax.nn.relu(m)
            aggr = jax.ops.segment_sum(m, dst, num_segments=n) * inv_cnt
            h = jnp.concatenate([aggr, x], axis=-1) @ agg_W[l] + agg_b[l]
            x = _l2norm(jax.nn.relu(h))
            if l < num_layers - 1:
                e = jnp.concatenate([x[src], x[dst], edge_attr], axis=-1) @ edge_W[l] + edge_b[l]
                edge_attr = jax.nn.relu(e)
        return x

    def _L3_gnn_ref(edge_index, embedding_weight):
        import jax, jax.numpy as jnp
        import numpy as np
        NUM_NODES = 50000
        EMBED_DIM = 64
        NUM_EDGES = 1250000
        NUM_LAYERS = 3
        row, col = (edge_index[0], edge_index[1])
        n = embedding_weight.shape[0]
        deg = jax.ops.segment_sum(jnp.ones_like(row, dtype=embedding_weight.dtype), row, num_segments=n)
        deg_inv_sqrt = jnp.where(deg > 0, jax.lax.rsqrt(jnp.maximum(deg, 1.0)) * jnp.where(deg > 0, 1.0, 0.0) + jax.lax.rsqrt(jnp.maximum(deg, 1.0)) * 0.0, 0.0)
        deg_inv_sqrt = jnp.where(deg > 0, jax.lax.rsqrt(jnp.maximum(deg, 1.0)), 0.0)
        x = embedding_weight
        acc = x
        for _ in range(NUM_LAYERS):
            m = deg_inv_sqrt[row][:, None] * x[col]
            x = jax.ops.segment_sum(m, row, num_segments=n) * deg_inv_sqrt[:, None]
            acc = acc + x
        return acc / (NUM_LAYERS + 1)
    edge_index = jnp.stack([src, dst])
    x = _layernorm(x + _L0_gnn_ref(x, edge_index, edge_attr_16, L0_gnn_W_node, L0_gnn_W_edge, L0_gnn_attn_src, L0_gnn_attn_dst, L0_gnn_ln_gamma, L0_gnn_ln_beta), axis=-1)
    x = _layernorm(x + _L1_gnn_ref(x, src, dst), axis=-1)
    x = _layernorm(x + _L2_gnn_ref(x, edge_attr_64, edge_index, L2_gnn_msg_W, L2_gnn_msg_b, L2_gnn_agg_W, L2_gnn_agg_b, L2_gnn_edge_W, L2_gnn_edge_b), axis=-1)
    x = _layernorm(x + _L3_gnn_ref(edge_index, x), axis=-1)
    return x

_drawn_inputs = setup_inputs


def setup_inputs(seed=0):
    import zlib

    import numpy as np

    out = dict(_drawn_inputs(seed))
    spreads = {'L0_gnn_ln_gamma': (1.0, 0.2),
     'L0_gnn_ln_beta': (0.0, 0.1),
     'L2_gnn_msg_b': (0.0, 0.1),
     'L2_gnn_agg_b': (0.0, 0.1),
     'L2_gnn_edge_b': (0.0, 0.1)}
    factors = {}
    for name, (base, spread) in spreads.items():
        noise = np.random.default_rng([zlib.crc32(name.encode()), seed]).standard_normal(out[name].shape)
        drawn = base * np.exp(spread * noise) if base else spread * noise
        out[name] = jnp.asarray(drawn.astype(out[name].dtype))
    for name, factor in factors.items():
        out[name] = (out[name] * factor).astype(out[name].dtype)
    return out
```

```python
import concourse.bass as bass
from concourse import mybir
from contextlib import ExitStack

F32, BF16, F16, I32 = mybir.dt.float32, mybir.dt.bfloat16, mybir.dt.float16, mybir.dt.int32
ALU = mybir.AluOpType
ACT = mybir.ActivationFunctionType
AX = mybir.AxisListType
P = 128
J = 4
CH = P * J
W = 32
D = 64
H = 4
HD = D // H


class Shapes:

    def __init__(self, n, e):
        self.N, self.E = n, e
        self.NB = -(-(n + W - 1) // P)
        self.NP = self.NB * P
        self.NF = n // P
        self.NR = n - self.NF * P
        self.T = -(-e // CH)
        self.TF = e // CH
        self.TR = e - self.TF * CH
        assert self.T == self.TF + 1 and self.TR > 0


def later(t, ring):
    return not (isinstance(t, int) and t < ring)


def pipeline(eng, n, stages):
    def turn(i, q0):
        for lag, step in stages:
            q, borrow = (q0 - lag) % 4, (q0 - lag) // 4
            if isinstance(i, int):
                t = 4 * i + q0 - lag
                if 0 <= t < n:
                    step(t, q, t // 4)
            else:
                step(4 * i + (q0 - lag), q, i + borrow)

    last = (n - 1) // 4
    for t in range(8):
        turn(t // 4, t % 4)
    with eng.Fori(2, last) as i:
        for q0 in range(4):
            turn(i, q0)
    for t in range(4 * last, n + max(lag for lag, _ in stages)):
        turn(t // 4, t % 4)


def blocks(eng, n, step):
    for u in (0, 1):
        step(u, u, 0)
    if n // 2 > 1:
        with eng.Fori(1, n // 2) as i:
            for u in (0, 1):
                step(2 * i + u, u, i)
    if n % 2:
        step(n - 1, 0, n // 2)


class Chain:

    def __init__(self, eng, sem):
        self.eng, self.sem, self.n = eng, sem, 0

    def __call__(self, ins):
        self.n += 1
        ins.then_inc(self.sem, 1)
        self.eng.wait_ge(self.sem, self.n)


def phase_semaphores(nc, ctx, tag=""):
    taken = []

    def sem(name):
        taken.append(nc.alloc_semaphore(name=name + tag))
        return taken[-1]

    def close():
        nc.clear_and_free_semaphores(taken)
        nc.all_engine_barrier()
    ctx.callback(close)
    return sem


def node_view(dram, s):
    return dram.rearrange("(b p) c -> p b c", p=P)


def setup_phase(nc, S, G, x, src, dst, copies):
    TB = -(-S.T // P)
    with ExitStack() as ctx:
        sb = lambda name, shape, dt: ctx.enter_context(nc.sbuf_tensor(name, shape, dt))
        sem = phase_semaphores(nc, ctx)
        rows_i = sb("rows_i", [P, 2, TB, CH], I32)
        rows_f = sb("rows_f", [P, 2, TB, CH], F32)
        base_col = sb("base_col", [P, TB], F32)
        src_f = sb("src_f", [P, S.T, J], F32)
        blk_i = sb("blk_i", [P, S.T, J], I32)
        blk_f = sb("blk_f", [P, S.T, J], F32)
        valid = sb("valid", [P, S.T, J], F32)
        tmp = sb("tmp", [P, S.T, J], F32)
        ps = [ctx.enter_context(nc.psum_tensor(f"ps_set{i}", [P, 512], F32)) for i in range(2)]
        idx_clear, idx_in, x_in, x_clear, rows_ready = sem("idx_clear"), sem("idx_in"), sem("x_in"), sem("x_clear"), sem("rows_ready")
        ident_z, ident_ok, iotas, turned, moved, vch = sem("ident_z"), sem("ident_ok"), sem("iotas"), sem("turned"), sem("moved"), sem("vch")
        w_clear, w_in = sem("w_clear"), sem("w_in")
        last = S.TF - (TB - 1) * P
        with nc.Block() as block:
            @block.sync
            def _(sp):
                sp.wait_ge(idx_clear, 2)
                for k, a in enumerate((src, dst)):
                    for b in range(TB):
                        rows = min(P, S.TF - b * P)
                        sp.dma_start(rows_i[0:rows, k, b, :],
                                     a[b * P * CH:(b * P + rows) * CH].rearrange("(t e) -> t e", e=CH)).then_inc(idx_in, 16)
                    sp.dma_start(rows_i[last:last + 1, k, TB - 1, 0:S.TR],
                                 a[S.TF * CH:S.E].rearrange("(t e) -> t e", t=1)).then_inc(idx_in, 16)
                sp.dma_start(G.base_i[0:1, 0:S.TF],
                             dst[0:S.TF * CH].rearrange("(o t e) -> o t e", o=1, e=CH)[:, :, 0], allow_slow_non_contiguous=True).then_inc(idx_in, 16)
                sp.dma_start(G.base_i[0:1, S.TF:S.T], dst[S.TF * CH:S.TF * CH + 1].rearrange("(t e) -> t e", t=1)).then_inc(idx_in, 16)
                sp.wait_ge(x_clear, 1)
                sp.dma_start(G.x[:, 0:S.NF, :], x[0:S.NF * P, :].rearrange("(b p) c -> p b c", p=P)).then_inc(x_in, 16)
                sp.dma_start(G.x[0:S.NR, S.NF, :], x[S.NF * P:S.N, :]).then_inc(x_in, 16)
                sp.wait_ge(x_in, 32)

            @block.gpsimd
            def _(pool):
                pool.memset(G.ident[:, :], 0.0).then_inc(ident_z, 1)
                pool.memset(G.blockmask[:, :, :], 1.0).then_inc(ident_z, 1)
                pool.iota(G.iota_w[:, :], [[1, W]], base=0, channel_multiplier=0, allow_small_or_imprecise_dtypes=True).then_inc(iotas, 1)
                pool.iota(G.iota_p[:, :], [[1, P]], base=0, channel_multiplier=0, allow_small_or_imprecise_dtypes=True).then_inc(iotas, 1)
                pool.iota(G.iota_key[:, :], [[1, S.NB * W]], base=0, channel_multiplier=0, allow_small_or_imprecise_dtypes=True).then_inc(iotas, 1)
                pool.wait_ge(ident_z, 2)
                pool.affine_select(out=G.ident[:, :], in_=G.ident[:, :], compare_op=ALU.not_equal, fill=1.0, base=0,
                                   pattern=[[-1, P]], channel_multiplier=1).then_inc(ident_ok, 1)
                pool.affine_select(out=G.blockmask[:, :, 0], in_=G.blockmask[:, :, 0], compare_op=ALU.is_ge, fill=0.0, base=0,
                                   pattern=[[-W, J]], channel_multiplier=1).then_inc(ident_ok, 1)
                pool.wait_ge(ident_ok, 2)
                pool.affine_select(out=G.blockmask[:, :, 0], in_=G.blockmask[:, :, 0], compare_op=ALU.is_ge, fill=0.0, base=W - 1,
                                   pattern=[[W, J]], channel_multiplier=-1).then_inc(ident_ok, 1)
                pool.wait_ge(ident_ok, 3)

            @block.vector
            def _(dve):
                dve.memset(rows_i[:, 0, :, :], 0).then_inc(idx_clear, 1)
                dve.memset(rows_i[:, 1, :, :], -1).then_inc(idx_clear, 1)
                dve.memset(G.x[:, :, :], 0.0).then_inc(x_clear, 1)
                dve.memset(G.weights[:, :], 0.0).then_inc(w_clear, 1)
                link = Chain(dve, vch)
                dve.wait_ge(idx_in, 16 * (2 * (TB + 1) + 2))
                link(dve.tensor_copy(rows_f[:, :, :, :], rows_i[:, :, :, :]))
                link(dve.tensor_copy(base_col[:, :], rows_f[:, 1, :, 0]))
                for b in range(TB):
                    link(dve.tensor_scalar(rows_f[:, 1, b, :], rows_f[:, 1, b, :], base_col[:, b:b + 1], None, ALU.subtract))
                dve.sem_inc(rows_ready, 1)
                n = 0
                for k, out in enumerate((src_f, G.rel)):
                    for b in range(TB):
                        rows = min(P, S.T - b * P)
                        for j in range(J):
                            dve.wait_ge(turned, n + 1)
                            dve.tensor_copy(out[:, b * P:b * P + rows, j], ps[n % 2][:, 0:rows]).then_inc(moved, 1)
                            n += 1
                dve.wait_ge(moved, n)
                link(dve.tensor_copy(G.src_i[:, :], src_f[:, :, :].rearrange("p t j -> p (t j)")))
                link(dve.tensor_scalar(blk_i[:, :, :], G.src_i[:, :].rearrange("p (t j) -> p t j", j=J), 7, None, ALU.arith_shift_right))
                link(dve.tensor_copy(blk_f[:, :, :], blk_i[:, :, :]))
                link(dve.tensor_scalar(tmp[:, :, :], blk_f[:, :, :], -float(P), None, ALU.mult))
                link(dve.tensor_tensor(G.src_r[:, :, :], src_f[:, :, :], tmp[:, :, :], ALU.add))
                link(dve.tensor_scalar(valid[:, :, :], G.rel[:, :, :], 0.0, None, ALU.is_ge))
                link(dve.tensor_scalar(tmp[:, :, :], G.rel[:, :, :], float(W), None, ALU.is_lt))
                link(dve.tensor_tensor(valid[:, :, :], valid[:, :, :], tmp[:, :, :], ALU.mult))
                link(dve.tensor_scalar(tmp[:, :, :], blk_f[:, :, :], float(W), 1.0, ALU.mult, ALU.add))
                link(dve.tensor_tensor(tmp[:, :, :], tmp[:, :, :], G.rel[:, :, :], ALU.add))
                link(dve.tensor_tensor(tmp[:, :, :], tmp[:, :, :], valid[:, :, :], ALU.mult))
                link(dve.tensor_scalar(G.key[:, :, :], tmp[:, :, :], -1.0, None, ALU.add))
                dve.wait_ge(ident_ok, 3)
                link(dve.tensor_tensor(G.stack_id[:, :], G.ident[:, 0:W], G.ident[:, W:2 * W], ALU.add))
                for j in range(2, J):
                    link(dve.tensor_tensor(G.stack_id[:, :], G.stack_id[:, :], G.ident[:, j * W:(j + 1) * W], ALU.add))
                link(dve.tensor_copy(G.ident_bf[:, :], G.ident[:, :]))
                link(dve.memset(G.ones_bf[:, :], 1.0))

            @block.scalar
            def _(act):
                act.wait_ge(w_clear, 1)
                for dst_ap, src_ap in copies:
                    act.dma_start(dst_ap, src_ap).then_inc(w_in, 16)
                act.wait_ge(w_in, 16 * len(copies))

            @block.tensor
            def _(pe):
                pe.wait_ge(ident_ok, 1)
                pe.wait_ge(rows_ready, 1)
                n = 0
                for k in range(2):
                    for b in range(TB):
                        rows = min(P, S.T - b * P)
                        for j in range(J):
                            if n >= 2:
                                pe.wait_ge(moved, n - 1)
                            pe.transpose(ps[n % 2][:, 0:rows],
                                         rows_f[0:rows, k, b, :].rearrange("t (p j) -> t p j", j=J)[:, :, j],
                                         G.ident[0:rows, 0:rows]).then_inc(turned, 1)
                            n += 1


def project_phase(nc, S, G, tag, wcat, wcols, outs):
    with ExitStack() as ctx:
        sb = lambda name, shape, dt: ctx.enter_context(nc.sbuf_tensor(name, shape, dt))
        sem = phase_semaphores(nc, ctx)
        staged = [sb(f"staged{tag}{u}", [P, D], F32) for u in (0, 1)]
        xT = [sb(f"xT{tag}{u}", [D + 1, P], F32) for u in (0, 1)]
        table = sb(f"tab{tag}", [P, S.NB, wcols], F32)
        ps_t = [ctx.enter_context(nc.psum_tensor(f"ps_t{tag}{u}", [P, 512], F32)) for u in (0, 1)]
        ps_m = [ctx.enter_context(nc.psum_tensor(f"ps_m{tag}{u}", [P, 512], F32)) for u in (0, 1)]
        st, tr, ev, mm, tb, out_done, ones, begun = (sem(n + tag) for n in ("st", "tr", "ev", "mm", "tb", "tab_out", "ones", "begun"))
        with nc.Block() as block:
            @block.sync
            def _(sp):
                sp.wait_ge(tb, S.NB)
                for c0, c1, dram in outs:
                    sp.dma_start(node_view(dram, S), table[:, :, c0:c1]).then_inc(out_done, 16)
                sp.wait_ge(out_done, 16 * len(outs))

            @block.gpsimd
            def _(pool):
                def stage(b, u, i):
                    if not (isinstance(i, int) and i == 0):
                        pool.wait_ge(tr, b - 1)
                    pool.tensor_copy(staged[u][:, :], G.x[:, bass.ds(b, 1), :].rearrange("p o c -> p (o c)")).then_inc(st, 1)
                blocks(pool, S.NB, stage)

            @block.tensor
            def _(pe):
                pe.wait_ge(ones, 2)

                def project(b, u, i):
                    pe.wait_ge(st, b + 1)
                    if not (isinstance(i, int) and i == 0):
                        pe.wait_ge(ev, b - 1)
                        pe.wait_ge(tb, b - 1)
                    pe.sem_inc(begun, 1)
                    pe.transpose(ps_t[u][0:D, 0:P], staged[u][:, :], G.ident[:, :]).then_inc(tr, 1)
                    pe.wait_ge(ev, b + 1)
                    pe.matmul(ps_m[u][:, 0:wcols], xT[u][:, :], wcat, start=True, stop=True).then_inc(mm, 1)
                blocks(pe, S.NB, project)

            @block.scalar
            def _(act):
                def evacuate(b, u, i):
                    act.wait_ge(tr, b + 1)
                    if not (isinstance(i, int) and i == 0):
                        act.wait_ge(mm, b - 1)
                    act.copy(xT[u][0:D, :], ps_t[u][0:D, 0:P]).then_inc(ev, 1)
                blocks(act, S.NB, evacuate)

            @block.vector
            def _(dve):
                for u in (0, 1):
                    dve.memset(xT[u][D:D + 1, :], 1.0).then_inc(ones, 1)

                def keep(b, u, i):
                    dve.wait_ge(mm, b + 1)
                    dve.tensor_copy(table[:, bass.ds(b, 1), :].rearrange("p o c -> p (o c)"), ps_m[u][:, 0:wcols]).then_inc(tb, 1)
                blocks(dve, S.NB, keep)


def attention_weights_phase(nc, S, G):
    with ExitStack() as ctx:
        sem = phase_semaphores(nc, ctx)
        wT = ctx.enter_context(nc.sbuf_tensor("wT", [D, D], F32))
        ps = ctx.enter_context(nc.psum_tensor("ps_aw", [P, 512], F32))
        aw_turned, aw_copied, aw_product, aw_done = sem("aw_turned"), sem("aw_copied"), sem("aw_product"), sem("aw_done")
        with nc.Block() as block:
            @block.tensor
            def _(pe):
                pe.transpose(ps[0:D, 0:D], G.w0[0:D, 0:D], G.ident[0:D, 0:D]).then_inc(aw_turned, 1)
                pe.wait_ge(aw_copied, 1)
                pe.matmul(ps[0:D, D:D + 2 * H], wT[:, :], G.w_attn[0:D, :], start=True, stop=True).then_inc(aw_product, 1)

            @block.vector
            def _(dve):
                dve.wait_ge(aw_turned, 1)
                dve.tensor_copy(wT[:, :], ps[0:D, 0:D]).then_inc(aw_copied, 1)
                dve.wait_ge(aw_product, 1)
                dve.tensor_copy(G.w0[0:D, D:D + 2 * H], ps[0:D, D:D + 2 * H]).then_inc(aw_done, 1)
                dve.wait_ge(aw_done, 1)


def window_copy(block_of_rows, base):
    rows = block_of_rows[bass.ds(base, W), :]
    return bass.AP(rows.tensor, rows.offset, [[0, J]] + [list(a) for a in rows.ap])


def scores_phase(nc, S, G, table0, tableA, edge_attr_16, gathered, max_table):
    C0 = D + H
    SPLIT = 512 // W
    with ExitStack() as ctx:
        sb = lambda name, shape, dt: ctx.enter_context(nc.sbuf_tensor(name, shape, dt))
        pb = lambda name, cols: ctx.enter_context(nc.psum_tensor(name, [P, cols], F32))
        sem = phase_semaphores(nc, ctx)
        ring = lambda f: [f(q) for q in range(4)]
        ea = ring(lambda q: sb(f"s_ea{q}", [P, J * 16], F32))
        ea_last = sb("s_ea_last", [P, J * 16], F32)
        eaT = ring(lambda q: sb(f"s_eaT{q}", [J * 16, P], F32))
        win = ring(lambda q: sb(f"s_win{q}", [P, H], F32))
        winbd = ring(lambda q: sb(f"s_winbd{q}", [P, J, H], F32))
        oh = ring(lambda q: sb(f"s_oh{q}", [P, J, W], F32))
        ohT = ring(lambda q: sb(f"s_ohT{q}", [P, P], F32))
        rows = ring(lambda q: sb(f"s_rows{q}", [P, J, C0], F32))
        index, index_ok = ring(lambda q: sb(f"s_index{q}", [P, J], I32)), sem("s_index")
        gathering, indexing = sem("s_gathering"), sem("s_indexing")
        masked = ring(lambda q: sb(f"s_masked{q}", [P, J, H, W], F32))
        score = ring(lambda q: sb(f"s_score{q}", [P, J, H], F32))
        mcol = ring(lambda q: sb(f"s_mcol{q}", [P, 1], F32))
        mdiag = ring(lambda q: sb(f"s_mdiag{q}", [P, W], F32))
        ohkey = [sb(f"s_ohkey{j}", [P, S.NB * W], F16) for j in range(J)]
        ohsrc = [sb(f"s_ohsrc{j}", [P, P], F16) for j in range(J)]
        ps_t, ps_s, ps_m, ps_w = (pb(n, 512) for n in ("ps_turned", "ps_scores", "ps_masked", "ps_window"))
        ps_a = [pb(f"ps_adj{u}", 1024) for u in (0, 1)]
        ea_in, win_in, rows_in, rows_out = (ring(lambda q: sem(f"s_{n}{q}")) for n in ("ea", "wi", "ri", "ro"))
        oh_ok, key_ok, src_ok, winbd_ok, turned, evac, scored, score_ok, attn_ok, masked_ok = (
            sem("s_" + n) for n in ("oh", "key", "src", "wbd", "turned", "evac", "scored", "score", "attn", "masked"))
        mask_turned, mcol_ok, mdiag_ok, window_max_ok, merged, adj_mm, adj_ok, cleared = (
            sem("s_" + n) for n in ("mturned", "mcol", "mdiag", "mwin", "merged", "adjmm", "adjok", "cleared"))
        max_turned, max_copied, max_out = sem("s_max_turned"), sem("s_max_copied"), sem("s_max_out")
        max_nodes = sb("s_max_nodes", [P, S.NB, H], F32)
        with nc.Block() as block:
            @block.sync
            def _(sp):
                def load(t, q, i):
                    if isinstance(t, int) and t == S.TF:
                        sp.wait_ge(cleared, 1)
                        sp.wait_ge(turned, 2 * (t - 3))
                        full, rest, e0 = S.TR // J, S.TR % J, S.TF * CH
                        sp.dma_start(ea_last[0:full, :], edge_attr_16[e0:e0 + full * J, :].rearrange("(p j) c -> p (j c)", j=J)).then_inc(ea_in[q], 16)
                        if rest:
                            sp.dma_start(ea_last[full:full + 1, 0:rest * 16],
                                         edge_attr_16[e0 + full * J:S.E, :].rearrange("(p j) c -> p (j c)", p=1)).then_inc(ea_in[q], 16)
                    else:
                        if later(t, 4):
                            sp.wait_ge(turned, 2 * (t - 3))
                        sp.dma_start(ea[q][:, :], edge_attr_16[bass.ds(t * CH, CH), :].rearrange("(p j) c -> p (j c)", j=J)).then_inc(ea_in[q], 16)
                    if later(t, 4):
                        sp.wait_ge(winbd_ok, t - 3)
                    base = sp.value_load(G.base_i[0:1, bass.ds(t, 1)], min_val=0, max_val=S.N - 1)
                    sp.dma_start(win[q][:, :], window_copy(tableA, base)).then_inc(win_in[q], 16)

                def store(t, q, i):
                    sp.wait_ge(attn_ok, t + 1)
                    sp.dma_start(gathered[bass.ds(t * P, P), :], rows[q][:, :, :].rearrange("p j c -> p (j c)")).then_inc(rows_out[q], 16)

                pipeline(sp, S.T, [(0, load), (2, store)])
                for q in range(4):
                    sp.wait_ge(rows_out[q], 16 * len(range(q, S.T, 4)))
                sp.wait_ge(max_copied, 1)
                sp.dma_start(node_view(max_table, S), max_nodes[:, :, :]).then_inc(max_out, 16)
                sp.wait_ge(max_out, 16)

            @block.gpsimd
            def _(pool):
                pool.memset(ea_last[:, :], 0.0).then_inc(cleared, 1)

                def take_index(t, q, i):
                    if later(t, 4):
                        pool.wait_ge(rows_in[q], 16 * J * i)
                    pool.sem_inc(indexing, 1)
                    pool.tensor_copy(index[q][:, :], G.src_i[:, bass.ds(t * J, J)]).then_inc(index_ok, 1)

                def gather(t, q, i):
                    pool.wait_ge(index_ok, t + 1)
                    if later(t, 4):
                        pool.wait_ge(masked_ok, t - 3)
                        pool.wait_ge(rows_out[q], 16 * i)
                    pool.sem_inc(gathering, 1)
                    for j in range(J):
                        pool.indirect_dma_start(rows[q][:, j, :], None, table0, bass.IndirectOffsetOnAxis(
                            ap=index[q][:, j:j + 1], axis=0)).then_inc(rows_in[q], 16)
                pipeline(pool, S.T, [(0, take_index), (1, gather)])

            @block.vector
            def _(dve):
                dve.memset(G.adj[:, :, :], 0.0).then_inc(adj_ok, 1)
                dve.memset(G.acc[:, :], 0.0).then_inc(merged, 1)

                def build(t, q, i):
                    if later(t, 4):
                        dve.wait_ge(turned, 2 * (t - 3))
                        dve.wait_ge(masked_ok, t - 3)
                    dve.tensor_tensor(oh[q][:, :, :], G.rel[:, bass.ds(t, 1), :].rearrange("p o j -> p (o j)").unsqueeze(2).broadcast_to([P, J, W]),
                                      G.iota_w[:, :].unsqueeze(1).broadcast_to([P, J, W]), ALU.is_equal).then_inc(oh_ok, 1)
                    dve.wait_ge(win_in[q], 16 * (i + 1))
                    if later(t, 4):
                        dve.wait_ge(scored, t - 3)
                    dve.tensor_tensor(winbd[q][:, :, :], win[q][:, :].unsqueeze(1).broadcast_to([P, J, H]),
                                      G.blockmask[:, :, :].broadcast_to([P, J, H]), ALU.mult).then_inc(winbd_ok, 1)
                    for j in range(J):
                        if later(t, 1):
                            dve.wait_ge(adj_mm, (t - 1) * J + j + 1)
                        dve.tensor_scalar(ohkey[j][:, :], G.iota_key[:, :], G.key[:, bass.ds(t, 1), j], None, ALU.is_equal).then_inc(key_ok, 1)
                        dve.tensor_scalar(ohsrc[j][:, :], G.iota_p[:, :], G.src_r[:, bass.ds(t, 1), j], None, ALU.is_equal).then_inc(src_ok, 1)

                def attend(t, q, i):
                    dve.wait_ge(scored, t + 1)
                    dve.wait_ge(rows_in[q], 16 * J * (i + 1))
                    dve.tensor_tensor(score[q][:, :, :], ps_s[:, 0:J * H].rearrange("p (j h) -> p j h", h=H),
                                      rows[q][:, :, D:C0], ALU.add).then_inc(score_ok, 1)
                    dve.wait_ge(score_ok, t + 1)
                    dve.scalar_tensor_tensor(rows[q][:, :, D:C0], score[q][:, :, :], 0.2, score[q][:, :, :], ALU.mult, ALU.max).then_inc(attn_ok, 1)
                    dve.wait_ge(attn_ok, t + 1)
                    if later(t, 4):
                        dve.wait_ge(mask_turned, J * (t - 3))
                    for j in range(J):
                        ins = dve.tensor_tensor(masked[q][:, j, :, :], rows[q][:, j, D:C0].unsqueeze(2).broadcast_to([P, H, W]),
                                                oh[q][:, j, :].unsqueeze(1).broadcast_to([P, H, W]), ALU.mult)
                    ins.then_inc(masked_ok, 1)

                def add_counts(t, q, i):
                    base = dve.value_load(G.base_i[0:1, bass.ds(t, 1)], min_val=0, max_val=S.N - 1)
                    dve.wait_ge(adj_mm, (t + 1) * J)
                    dve.wait_ge(adj_ok, t + 1)
                    window = G.adj[:, :, bass.ds(base, W)]
                    dve.tensor_tensor(window, window, ps_a[q % 2][:, 0:S.NB * W].rearrange("p (b w) -> p b w", w=W), ALU.add).then_inc(adj_ok, 1)

                def reduce(t, q, i):
                    dve.wait_ge(mask_turned, J * (t + 1))
                    dve.reduce_max(mcol[q][:, :], ps_m[:, :], axis=AX.X).then_inc(mcol_ok, 1)
                    dve.wait_ge(mcol_ok, t + 1)
                    if later(t, 4):
                        dve.wait_ge(window_max_ok, t - 3)
                    dve.tensor_scalar(mdiag[q][:, :], G.stack_id[:, :], mcol[q][:, 0:1], None, ALU.mult).then_inc(mdiag_ok, 1)

                def merge(t, q, i):
                    base = dve.value_load(G.base_i[0:1, bass.ds(t, 1)], min_val=0, max_val=S.N - 1)
                    dve.wait_ge(window_max_ok, t + 1)
                    dve.wait_ge(merged, t + 1)
                    window = G.acc[0:H, bass.ds(base, W)]
                    dve.tensor_tensor(window, window, ps_w[0:H, 0:W], ALU.max).then_inc(merged, 1)

                pipeline(dve, S.T, [(0, build), (1, attend), (1, add_counts), (2, reduce), (3, merge)])
                dve.wait_ge(max_turned, 1)
                dve.tensor_copy(max_nodes[:, :, :], ps_m[:, 0:S.NB * H].rearrange("p (b h) -> p b h", h=H)).then_inc(max_copied, 1)

            @block.scalar
            def _(act):
                def evacuate(t, q, i):
                    act.wait_ge(turned, 2 * (t + 1))
                    if later(t, 4):
                        act.wait_ge(scored, t - 3)
                    act.copy(ohT[q][:, :], ps_t[:, 0:P]).then_inc(evac, 1)
                    act.copy(eaT[q][:, :], ps_t[0:J * 16, P:2 * P]).then_inc(evac, 1)
                pipeline(act, S.T, [(0, evacuate)])

            @block.tensor
            def _(pe):
                def turn(t, q, i):
                    last = isinstance(t, int) and t == S.TF
                    pe.wait_ge(ea_in[q], 16 * (i + 1) + (16 if last and S.TR % J else 0))
                    pe.wait_ge(oh_ok, t + 1)
                    if later(t, 1):
                        pe.wait_ge(evac, 2 * t)
                    pe.transpose(ps_t[:, 0:P], oh[q][:, :, :].rearrange("p j w -> p (j w)"), G.ident[:, :]).then_inc(turned, 1)
                    pe.transpose(ps_t[0:J * 16, P:2 * P], (ea_last if last else ea[q])[:, :], G.ident[:, :]).then_inc(turned, 1)

                def count(t, q, i):
                    if later(t, 2):
                        pe.wait_ge(adj_ok, t)
                    for j in range(J):
                        pe.wait_ge(key_ok, t * J + j + 1)
                        pe.wait_ge(src_ok, t * J + j + 1)
                        for b0, b1 in ((0, min(SPLIT, S.NB)), (SPLIT, S.NB)):
                            if b1 > b0:
                                ins = pe.matmul(ps_a[q % 2][:, b0 * W:b1 * W], ohsrc[j][:, :], ohkey[j][:, b0 * W:b1 * W],
                                                start=(j == 0), stop=(j == J - 1))
                        ins.then_inc(adj_mm, 1)

                def score_edges(t, q, i):
                    pe.wait_ge(evac, 2 * (t + 1))
                    pe.wait_ge(winbd_ok, t + 1)
                    if later(t, 1):
                        pe.wait_ge(score_ok, t)
                    out = ps_s[:, 0:J * H]
                    pe.matmul(out, ohT[q][:, :], winbd[q][:, :, :].rearrange("p j h -> p (j h)"), start=True, stop=False)
                    pe.matmul(out, eaT[q][:, :], G.w_edge16[0:J * 16, :], start=False, stop=True).then_inc(scored, 1)

                def turn_masked(t, q, i):
                    pe.wait_ge(masked_ok, t + 1)
                    if later(t, 1):
                        pe.wait_ge(mcol_ok, t)
                    for j in range(J):
                        pe.transpose(ps_m[:, j * P:(j + 1) * P], masked[q][:, j, :, :].rearrange("p h w -> p (h w)"), G.ident[:, :]).then_inc(mask_turned, 1)

                def window_max(t, q, i):
                    pe.wait_ge(mdiag_ok, t + 1)
                    if later(t, 1):
                        pe.wait_ge(merged, t + 1)
                    pe.matmul(ps_w[0:H, 0:W], G.blockmask[:, :, 0], mdiag[q][:, :], start=True, stop=True).then_inc(window_max_ok, 1)

                pipeline(pe, S.T, [(0, turn), (0, count), (0, score_edges), (1, turn_masked), (2, window_max)])
                pe.wait_ge(merged, S.T + 1)
                pe.wait_ge(mcol_ok, S.T)
                for b in range(S.NB):
                    ins = pe.transpose(ps_m[:, b * H:(b + 1) * H], G.acc[0:H, b * P:(b + 1) * P], G.ident[0:H, 0:H])
                ins.then_inc(max_turned, 1)


def softmax_phase(nc, S, G, max_table, gathered):
    C0 = D + H
    with ExitStack() as ctx:
        sb = lambda name, shape, dt: ctx.enter_context(nc.sbuf_tensor(name, shape, dt))
        pb = lambda name, cols: ctx.enter_context(nc.psum_tensor(name, [P, cols], F32))
        sem = phase_semaphores(nc, ctx)
        ring = lambda f: [f(q) for q in range(4)]
        win = ring(lambda q: sb(f"x_win{q}", [P, H], F32))
        winbd = ring(lambda q: sb(f"x_winbd{q}", [P, J, H], F32))
        oh = ring(lambda q: sb(f"x_oh{q}", [P, J, W], F32))
        ohT = ring(lambda q: sb(f"x_ohT{q}", [P, P], F32))
        rows = ring(lambda q: sb(f"x_rows{q}", [P, J, C0], F32))
        arg = ring(lambda q: sb(f"x_arg{q}", [P, J, H], F32))
        msg = ring(lambda q: sb(f"x_msg{q}", [P, J, C0], F32))
        ps_t, ps_s, ps_w = ([pb(f"ps_x{n}{u}", 512) for u in (0, 1)] for n in "tsw")
        win_in, rows_in = (ring(lambda q: sem(f"x_{n}{q}")) for n in ("wi", "ri"))
        oh_ok, winbd_ok, turned, evac, spread, diff_ok, arg_ok, exp_ok, msg_ok, summed, added = (
            sem("x_" + n) for n in ("oh", "wbd", "turned", "evac", "spread", "diff", "arg", "exp", "msg", "summed", "added"))
        with nc.Block() as block:
            @block.sync
            def _(sp):
                def load(t, q, i):
                    if later(t, 4):
                        sp.wait_ge(msg_ok, t - 3)
                        sp.wait_ge(winbd_ok, t - 3)
                    sp.dma_start(rows[q][:, :, :].rearrange("p j c -> p (j c)"), gathered[bass.ds(t * P, P), :]).then_inc(rows_in[q], 16)
                    base = sp.value_load(G.base_i[0:1, bass.ds(t, 1)], min_val=0, max_val=S.N - 1)
                    sp.dma_start(win[q][:, :], window_copy(max_table, base)).then_inc(win_in[q], 16)
                pipeline(sp, S.T, [(0, load)])

            @block.vector
            def _(dve):
                dve.memset(G.acc[:, :], 0.0).then_inc(added, 1)

                def build(t, q, i):
                    if later(t, 4):
                        dve.wait_ge(summed, t - 3)
                    dve.tensor_tensor(oh[q][:, :, :], G.rel[:, bass.ds(t, 1), :].rearrange("p o j -> p (o j)").unsqueeze(2).broadcast_to([P, J, W]),
                                      G.iota_w[:, :].unsqueeze(1).broadcast_to([P, J, W]), ALU.is_equal).then_inc(oh_ok, 1)
                    dve.wait_ge(win_in[q], 16 * (i + 1))
                    dve.tensor_tensor(winbd[q][:, :, :], win[q][:, :].unsqueeze(1).broadcast_to([P, J, H]),
                                      G.blockmask[:, :, :].broadcast_to([P, J, H]), ALU.mult).then_inc(winbd_ok, 1)

                def exponent(t, q, i):
                    dve.wait_ge(spread, t + 1)
                    dve.wait_ge(rows_in[q], 16 * (i + 1))
                    dve.tensor_tensor(arg[q][:, :, :], rows[q][:, :, D:C0],
                                      ps_s[q % 2][:, 0:J * H].rearrange("p (j h) -> p j h", h=H), ALU.subtract).then_inc(diff_ok, 1)
                    dve.wait_ge(diff_ok, t + 1)
                    dve.tensor_scalar(arg[q][:, :, :], arg[q][:, :, :], 0.0, None, ALU.min).then_inc(arg_ok, 1)

                def weigh(t, q, i):
                    dve.wait_ge(exp_ok, t + 1)
                    dve.tensor_tensor(msg[q][:, :, 0:D].rearrange("p j (h d) -> p j h d", h=H),
                                      rows[q][:, :, 0:D].rearrange("p j (h d) -> p j h d", h=H),
                                      msg[q][:, :, D:C0].unsqueeze(3).broadcast_to([P, J, H, HD]), ALU.mult).then_inc(msg_ok, 1)

                def add(t, q, i):
                    base = dve.value_load(G.base_i[0:1, bass.ds(t, 1)], min_val=0, max_val=S.N - 1)
                    dve.wait_ge(summed, t + 1)
                    dve.wait_ge(added, t + 1)
                    window = G.acc[0:C0, bass.ds(base, W)]
                    dve.tensor_tensor(window, window, ps_w[q % 2][0:C0, 0:W], ALU.add).then_inc(added, 1)
                pipeline(dve, S.T, [(0, build), (1, exponent), (2, weigh), (3, add)])
                dve.wait_ge(added, S.T + 1)

            @block.scalar
            def _(act):
                def evacuate(t, q, i):
                    act.wait_ge(turned, t + 1)
                    if later(t, 4):
                        act.wait_ge(spread, t - 3)
                    act.copy(ohT[q][:, :], ps_t[q % 2][:, 0:P]).then_inc(evac, 1)

                def exponential(t, q, i):
                    act.wait_ge(arg_ok, t + 1)
                    if later(t, 4):
                        act.wait_ge(summed, t - 3)
                        act.wait_ge(msg_ok, t - 3)
                    act.activation(msg[q][:, :, D:C0], arg[q][:, :, :], ACT.Exp).then_inc(exp_ok, 1)
                pipeline(act, S.T, [(0, evacuate), (1, exponential)])

            @block.tensor
            def _(pe):
                def turn(t, q, i):
                    pe.wait_ge(oh_ok, t + 1)
                    if later(t, 2):
                        pe.wait_ge(evac, t - 1)
                    pe.transpose(ps_t[q % 2][:, 0:P], oh[q][:, :, :].rearrange("p j w -> p (j w)"), G.ident[:, :]).then_inc(turned, 1)

                def spread_max(t, q, i):
                    pe.wait_ge(evac, t + 1)
                    pe.wait_ge(winbd_ok, t + 1)
                    if later(t, 2):
                        pe.wait_ge(diff_ok, t - 1)
                    pe.matmul(ps_s[q % 2][:, 0:J * H], ohT[q][:, :], winbd[q][:, :, :].rearrange("p j h -> p (j h)"),
                              start=True, stop=True).then_inc(spread, 1)

                def scatter(t, q, i):
                    pe.wait_ge(msg_ok, t + 1)
                    if later(t, 2):
                        pe.wait_ge(added, t)
                    for j in range(J):
                        ins = pe.matmul(ps_w[q % 2][0:C0, 0:W], msg[q][:, j, :], oh[q][:, j, :], start=(j == 0), stop=(j == J - 1))
                    ins.then_inc(summed, 1)
                pipeline(pe, S.T, [(0, turn), (0, spread_max), (2, scatter)])


def attention_nodes_phase(nc, S, G, table0):
    C0 = D + H
    PER = 512 // C0
    NG = -(-S.NB // PER)
    with ExitStack() as ctx:
        sb = lambda name, shape, dt: ctx.enter_context(nc.sbuf_tensor(name, shape, dt))
        sem = phase_semaphores(nc, ctx)
        h = sb("n_h", [P, S.NB, D], F32)
        sums = sb("n_sums", [P, S.NB, C0], F32)
        ps = [ctx.enter_context(nc.psum_tensor(f"ps_n{g}", [P, 512], F32)) for g in range(NG)]
        h_in, turned, chain = sem("n_h_in"), sem("n_turned"), sem("n_chain")
        with nc.Block() as block:
            @block.sync
            def _(sp):
                sp.dma_start(h[:, :, :], node_view(table0, S)[:, :, 0:D]).then_inc(h_in, 16)
                sp.wait_ge(h_in, 16)

            @block.tensor
            def _(pe):
                for b in range(S.NB):
                    g, k = divmod(b, PER)
                    pe.transpose(ps[g][:, k * C0:(k + 1) * C0], G.acc[0:C0, b * P:(b + 1) * P], G.ident[0:C0, 0:C0]).then_inc(turned, 1)

            @block.vector
            def _(dve):
                link = Chain(dve, chain)
                for g in range(NG):
                    b0, b1 = g * PER, min((g + 1) * PER, S.NB)
                    dve.wait_ge(turned, b1)
                    link(dve.tensor_copy(sums[:, b0:b1, :], ps[g][:, 0:(b1 - b0) * C0].rearrange("p (b c) -> p b c", c=C0)))
                link(dve.tensor_scalar(sums[:, :, D:C0], sums[:, :, D:C0], 1e-8, None, ALU.add))
                link(dve.reciprocal(sums[:, :, D:C0], sums[:, :, D:C0]))
                for k in range(H):
                    link(dve.tensor_tensor(G.y[:, :, k * HD:(k + 1) * HD], sums[:, :, k * HD:(k + 1) * HD],
                                           sums[:, :, D + k:D + k + 1].broadcast_to([P, S.NB, HD]), ALU.mult))
                dve.wait_ge(h_in, 16)
                link(dve.tensor_tensor(G.y[:, :, :], G.y[:, :, :], h[:, :, :], ALU.add))


def norm_phase(nc, S, G, tag, affine, out):
    with ExitStack() as ctx:
        sb = lambda name, shape, dt: ctx.enter_context(nc.sbuf_tensor(name + tag, shape, dt))
        sem = phase_semaphores(nc, ctx, tag)
        centred, square = sb("centred", [P, S.NB, D], F32), sb("square", [P, S.NB, D], F32)
        mean, var, std, inv = (sb(n, [P, S.NB], F32) for n in ("mean", "var", "std", "inv"))
        chain, var_ok, std_ok = sem("nchain"), sem("var_ok"), sem("std_ok")
        wide = lambda a: a[:, :].unsqueeze(2).broadcast_to([P, S.NB, D])
        with nc.Block() as block:
            @block.vector
            def _(dve):
                link = Chain(dve, chain)
                link(dve.reduce_sum(mean[:, :], G.y[:, :, :], axis=AX.X))
                link(dve.tensor_scalar(mean[:, :], mean[:, :], 1.0 / D, None, ALU.mult))
                link(dve.tensor_tensor(centred[:, :, :], G.y[:, :, :], wide(mean), ALU.subtract))
                link(dve.tensor_tensor(square[:, :, :], centred[:, :, :], centred[:, :, :], ALU.mult))
                link(dve.reduce_sum(var[:, :], square[:, :, :], axis=AX.X))
                link(dve.tensor_scalar(var[:, :], var[:, :], 1.0 / D, 1e-5, ALU.mult, ALU.add))
                dve.sem_inc(var_ok, 1)
                dve.wait_ge(std_ok, 1)
                link(dve.reciprocal(inv[:, :], std[:, :]))
                if affine:
                    link(dve.tensor_tensor(centred[:, :, :], centred[:, :, :], wide(inv), ALU.mult))
                    row = lambda a: a.unsqueeze(1).broadcast_to([P, S.NB, D])
                    link(dve.tensor_tensor(centred[:, :, :], centred[:, :, :], row(G.gamma), ALU.mult))
                    link(dve.tensor_tensor(centred[:, :, :], centred[:, :, :], row(G.beta), ALU.add))
                    link(dve.tensor_tensor(out[:, :, :], centred[:, :, :], G.x[:, :, :], ALU.add))
                else:
                    link(dve.tensor_tensor(out[:, :, :], centred[:, :, :], wide(inv), ALU.mult))

            @block.scalar
            def _(act):
                act.wait_ge(var_ok, 1)
                act.activation(std[:, :], var[:, :], ACT.Sqrt).then_inc(std_ok, 1)


def widen_block(eng, copy, S, adj, wide, m, b0, b1):
    return copy(wide[:, b0:b1, :], adj[:, b0:b1, bass.ds(m * P, P)])


def propagate_phase(nc, S, G, tag, adj, theta, room):
    AB = (S.NB + 1) // 2
    with ExitStack() as ctx:
        sem = phase_semaphores(nc, ctx, tag)
        parts = room("parts" + tag, [P, S.NB, 3 * D], BF16)
        agg, rest, feat = (room(n + tag, [P, S.NB, D], F32) for n in ("agg", "rest", "feat"))
        deg, dinv = room("deg" + tag, [P, S.NB], F32), room("dinv" + tag, [P, S.NB], F32)
        wide_adj = [room(f"wide{u}" + tag, [P, S.NB, P], BF16) for u in (0, 1)]
        ps = [ctx.enter_context(nc.psum_tensor(f"ps_p{tag}{u}", [P, 512], F32)) for u in (0, 1)]
        chain, deg_ok, sqrt_ok, parts_ok, product, taken, by_act, by_dve = (
            sem(n) for n in ("pchain", "deg_ok", "sqrt_ok", "parts_ok", "product", "taken", "by_act", "by_dve"))
        wide = lambda a: a[:, :].unsqueeze(2).broadcast_to([P, S.NB, D])
        first = lambda k, i: k == 0 and isinstance(i, int) and i == 0
        with nc.Block() as block:
            @block.tensor
            def _(pe):
                for k in range(4):
                    if k:
                        pe.wait_ge(parts_ok, k)

                    def multiply(m, u, i):
                        n = k * S.NB + m
                        if not (isinstance(i, int) and i == 0):
                            pe.wait_ge(taken, n - 1)
                        elif k:
                            pe.wait_ge(taken, k * S.NB)
                        pe.wait_ge(by_dve, n + 1)
                        pe.wait_ge(by_act, n + 1)
                        for b in range(S.NB):
                            ins = pe.matmul(ps[u][:, 0:3 * D] if k else ps[u][:, 0:1], wide_adj[u][:, b, :],
                                            parts[:, b, :] if k else G.ones_bf[:, 0:1], start=(b == 0), stop=(b == S.NB - 1))
                        ins.then_inc(product, 1)
                    blocks(pe, S.NB, multiply)

            @block.scalar
            def _(act):
                for k in range(4):
                    def widen(m, u, i):
                        n = k * S.NB + m
                        if not (isinstance(i, int) and i == 0):
                            act.wait_ge(product, n - 1)
                        elif k:
                            act.wait_ge(product, k * S.NB)
                        widen_block(act, act.copy, S, adj, wide_adj[u], m, 0, AB).then_inc(by_act, 1)
                    blocks(act, S.NB, widen)
                    if k == 0:
                        act.wait_ge(deg_ok, 1)
                        act.activation(dinv[:, :], deg[:, :], ACT.Sqrt).then_inc(sqrt_ok, 1)

            @block.vector
            def _(dve):
                link = Chain(dve, chain)

                def widen(k, m, u, i):
                    n = k * S.NB + m
                    if not (isinstance(i, int) and i == 0):
                        dve.wait_ge(product, n - 1)
                    elif k:
                        dve.wait_ge(product, k * S.NB)
                    widen_block(dve, dve.tensor_copy, S, adj, wide_adj[u], m, AB, S.NB).then_inc(by_dve, 1)

                def take(k, m, u):
                    dve.wait_ge(product, k * S.NB + m + 1)
                    if k:
                        dve.reduce_sum(agg[:, bass.ds(m, 1), :].rearrange("p o c -> p (o c)"),
                                       ps[u][:, 0:3 * D].rearrange("p (s c) -> p c s", c=D), axis=AX.X).then_inc(taken, 1)
                    else:
                        dve.tensor_copy(deg[:, bass.ds(m, 1)], ps[u][:, 0:1]).then_inc(taken, 1)

                for k in range(4):
                    def step(m, u, i):
                        widen(k, m, u, i)
                        if isinstance(m, int) and m == 0:
                            return
                        take(k, m - 1, 1 - u)
                    blocks(dve, S.NB, step)
                    take(k, S.NB - 1, (S.NB - 1) % 2)
                    dve.wait_ge(taken, (k + 1) * S.NB)
                    if k == 0:
                        link(dve.tensor_scalar(agg[:, 0, 0:S.NB], deg[:, :], 0.0, None, ALU.is_gt))
                        link(dve.tensor_scalar(deg[:, :], deg[:, :], 1.0, None, ALU.max))
                        dve.sem_inc(deg_ok, 1)
                        dve.wait_ge(sqrt_ok, 1)
                        link(dve.reciprocal(dinv[:, :], dinv[:, :]))
                        link(dve.tensor_copy(feat[:, :, :], G.x[:, :, :]))
                        if theta:
                            link(dve.reciprocal(G.inv_cnt[:, :], deg[:, :]))
                            link(dve.tensor_scalar(G.y[:, :, :], G.x[:, :, :], 1.0 + theta[0], None, ALU.mult))
                        else:
                            link(dve.tensor_tensor(dinv[:, :], dinv[:, :], agg[:, 0, 0:S.NB], ALU.mult))
                            link(dve.tensor_copy(G.y[:, :, :], G.x[:, :, :]))
                    else:
                        link(dve.tensor_tensor(agg[:, :, :], agg[:, :, :], wide(dinv), ALU.mult))
                        if theta:
                            link(dve.tensor_tensor(feat[:, :, :], feat[:, :, :], agg[:, :, :], ALU.subtract))
                            link(dve.scalar_tensor_tensor(G.y[:, :, :], feat[:, :, :], theta[k], G.y[:, :, :], ALU.mult, ALU.add))
                        else:
                            link(dve.tensor_tensor(feat[:, :, :], agg[:, :, :], wide(dinv), ALU.mult))
                            link(dve.tensor_tensor(G.y[:, :, :], G.y[:, :, :], feat[:, :, :], ALU.add))
                    if k == 3:
                        break
                    if theta:
                        link(dve.tensor_tensor(rest[:, :, :], feat[:, :, :], wide(dinv), ALU.mult))
                    else:
                        link(dve.tensor_copy(rest[:, :, :], feat[:, :, :]))
                    link(dve.tensor_copy(parts[:, :, 0:D], rest[:, :, :]))
                    link(dve.tensor_tensor(rest[:, :, :], rest[:, :, :], parts[:, :, 0:D], ALU.subtract))
                    link(dve.tensor_copy(parts[:, :, D:2 * D], rest[:, :, :]))
                    link(dve.tensor_tensor(rest[:, :, :], rest[:, :, :], parts[:, :, D:2 * D], ALU.subtract))
                    link(dve.tensor_copy(parts[:, :, 2 * D:3 * D], rest[:, :, :]))
                    dve.sem_inc(parts_ok, 1)
                if not theta:
                    link(dve.scalar_tensor_tensor(G.y[:, :, :], G.y[:, :, :], 0.25, G.x[:, :, :], ALU.mult, ALU.add))


def transpose_counts_phase(nc, S, G, adj, adjT):
    PER = 4
    NG = -(-S.NB // PER)
    AB = (S.NB + 1) // 2
    with ExitStack() as ctx:
        sem = phase_semaphores(nc, ctx)
        ps = [ctx.enter_context(nc.psum_tensor(f"ps_tc{g}", [P, 512], F32)) for g in range(NG)]
        wide_adj = ctx.enter_context(nc.sbuf_tensor("tc_wide", [P, S.NB, P], BF16))
        wide_act, wide_dve, turned, by_act, by_dve = (sem("tc_" + n) for n in ("wide_act", "wide_dve", "turned", "by_act", "by_dve"))
        n_act, n_dve = len(range(0, NG, 2)), len(range(1, NG, 2))

        def evacuate(eng, copy, done, widened, first, b0, b1):
            def step(m, u, i):
                if later(m, 1):
                    eng.wait_ge(turned, m * NG)
                widen_block(eng, copy, S, adj, wide_adj, m, b0, b1).then_inc(widened, 1)
                for g in range(first, NG, 2):
                    c0, c1 = g * PER, min((g + 1) * PER, S.NB)
                    eng.wait_ge(turned, m * NG + g + 1)
                    copy(adjT[:, bass.ds(m, 1), c0 * P:c1 * P].rearrange("p o c -> p (o c)"), ps[g][:, 0:(c1 - c0) * P]).then_inc(done, 1)
            blocks(eng, S.NB, step)

        with nc.Block() as block:
            @block.tensor
            def _(pe):
                def step(m, u, i):
                    pe.wait_ge(wide_act, m + 1)
                    pe.wait_ge(wide_dve, m + 1)
                    for g in range(NG):
                        if later(m, 1):
                            if g % 2:
                                pe.wait_ge(by_dve, (m - 1) * n_dve + g // 2 + 1)
                            else:
                                pe.wait_ge(by_act, (m - 1) * n_act + g // 2 + 1)
                        for b in range(g * PER, min((g + 1) * PER, S.NB)):
                            ins = pe.matmul(ps[g][:, (b % PER) * P:(b % PER + 1) * P], wide_adj[:, b, :], G.ident_bf[:, :],
                                            start=True, stop=True)
                        ins.then_inc(turned, 1)
                blocks(pe, S.NB, step)

            @block.scalar
            def _(act):
                evacuate(act, act.copy, by_act, wide_act, 0, 0, AB)

            @block.vector
            def _(dve):
                evacuate(dve, dve.tensor_copy, by_dve, wide_dve, 1, AB, S.NB)


def edge_phase(nc, S, G, tag, table, cols, target_table, w_edge, w_msg, edges, edges_transposed, keep):
    update = target_table is not None
    with ExitStack() as ctx:
        sb = lambda name, shape, dt: ctx.enter_context(nc.sbuf_tensor(name + tag, shape, dt))
        pb = lambda name: ctx.enter_context(nc.psum_tensor(name + tag, [P, 512], F32))
        sem = phase_semaphores(nc, ctx, tag)
        ring = lambda f: [f(q) for q in range(4)]
        C = J * D
        half = lambda a, k: a[:, k * P:(k + 1) * P]
        ea = ring(lambda q: sb(f"e_ea{q}", [P, C], F32)) if edges is not None else None
        ea_last = sb("e_ea_last", [P, C], F32) if edges is not None else None
        eaT = ring(lambda q: sb(f"e_eaT{q}", [P, C], F32))
        rows = ring(lambda q: sb(f"e_rows{q}", [P, J, cols], F32))
        index, index_ok = ring(lambda q: sb(f"e_index{q}", [P, J], I32)), sem("e_index")
        gathering, indexing = sem("e_gathering"), sem("e_indexing")
        oh = ring(lambda q: sb(f"e_oh{q}", [P, J, W], F32))
        ohT = ring(lambda q: sb(f"e_ohT{q}", [P, P], F32)) if update else None
        win = ring(lambda q: sb(f"e_win{q}", [P, D], F32)) if update else None
        winbd = ring(lambda q: sb(f"e_winbd{q}", [P, J, D], F32)) if update else None
        new = ring(lambda q: sb(f"e_new{q}", [P, J, D], F32)) if update else None
        newT = ring(lambda q: sb(f"e_newT{q}", [P, C], F32)) if update else eaT
        msg = ring(lambda q: sb(f"e_msg{q}", [P, J, D], F32))
        ps_t = [pb(f"ps_t{u}") for u in (0, 1)]
        ps_u = [pb(f"ps_u{u}") for u in (0, 1)]
        ps_m = [pb(f"ps_m{u}") for u in (0, 1)]
        ps_n, ps_w = pb("ps_n"), pb("ps_w")
        ea_in, eaT_in, win_in, rows_in, kept = (ring(lambda q: sem(f"e_{n}{q}_")) for n in ("ea", "eT", "wi", "ri", "kp"))
        oh_ok, winbd_ok, oh_turned, ea_turned, ohT_ok, eaT_ok, updated, new_pre, new_ok = (
            sem("e_" + n + "_") for n in ("oh", "wbd", "oht", "eat", "ohTo", "eaTo", "upd", "npre", "new"))
        new_turned, newT_ok, msg_mm, msg_pre, msg_ok, summed, added, cleared = (
            sem("e_" + n + "_") for n in ("nt", "nTo", "mm", "mpre", "msg", "sum", "add", "clr"))

        def wait_eaT(eng, t, q, i):
            if edges is None:
                eng.wait_ge(eaT_in[q], 16 * (i + 1))
            else:
                eng.wait_ge(eaT_ok, t + 1)

        with nc.Block() as block:
            @block.sync
            def _(sp):
                def load(t, q, i):
                    if edges is None:
                        if later(t, 4):
                            sp.wait_ge(updated, t - 3)
                        sp.dma_start(eaT[q][:, :], edges_transposed[bass.ds(t * P, P), :]).then_inc(eaT_in[q], 16)
                    elif isinstance(t, int) and t == S.TF:
                        sp.wait_ge(cleared, 1)
                        sp.wait_ge(ea_turned, t - 3)
                        full, rest, e0 = S.TR // J, S.TR % J, S.TF * CH
                        sp.dma_start(ea_last[0:full, :], edges[e0:e0 + full * J, :].rearrange("(p j) c -> p (j c)", j=J)).then_inc(ea_in[q], 16)
                        if rest:
                            sp.dma_start(ea_last[full:full + 1, 0:rest * D],
                                         edges[e0 + full * J:S.E, :].rearrange("(p j) c -> p (j c)", p=1)).then_inc(ea_in[q], 16)
                    else:
                        if later(t, 4):
                            sp.wait_ge(ea_turned, t - 3)
                        sp.dma_start(ea[q][:, :], edges[bass.ds(t * CH, CH), :].rearrange("(p j) c -> p (j c)", j=J)).then_inc(ea_in[q], 16)
                    if update:
                        if later(t, 4):
                            sp.wait_ge(winbd_ok, t - 3)
                        base = sp.value_load(G.base_i[0:1, bass.ds(t, 1)], min_val=0, max_val=S.N - 1)
                        sp.dma_start(win[q][:, :], window_copy(target_table, base)).then_inc(win_in[q], 16)

                def store(t, q, i):
                    sp.wait_ge(newT_ok, t + 1)
                    sp.dma_start(keep[bass.ds(t * P, P), :], newT[q][:, :]).then_inc(kept[q], 16)
                pipeline(sp, S.T, [(0, load)] + ([(3, store)] if keep is not None else []))
                if keep is not None:
                    for q in range(4):
                        sp.wait_ge(kept[q], 16 * len(range(q, S.T, 4)))

            @block.gpsimd
            def _(pool):
                if edges is not None:
                    pool.memset(ea_last[:, :], 0.0).then_inc(cleared, 1)

                def take_index(t, q, i):
                    if later(t, 4):
                        pool.wait_ge(rows_in[q], 16 * J * i)
                    pool.sem_inc(indexing, 1)
                    pool.tensor_copy(index[q][:, :], G.src_i[:, bass.ds(t * J, J)]).then_inc(index_ok, 1)

                def gather(t, q, i):
                    pool.wait_ge(index_ok, t + 1)
                    if later(t, 4):
                        pool.wait_ge(msg_pre, t - 3)
                    pool.sem_inc(gathering, 1)
                    for j in range(J):
                        pool.indirect_dma_start(rows[q][:, j, :], None, table, bass.IndirectOffsetOnAxis(
                            ap=index[q][:, j:j + 1], axis=0)).then_inc(rows_in[q], 16)
                pipeline(pool, S.T, [(0, take_index), (1, gather)])

            @block.vector
            def _(dve):
                dve.memset(G.acc[:, :], 0.0).then_inc(added, 1)

                def build(t, q, i):
                    if later(t, 4):
                        dve.wait_ge(summed, t - 3)
                    dve.tensor_tensor(oh[q][:, :, :], G.rel[:, bass.ds(t, 1), :].rearrange("p o j -> p (o j)").unsqueeze(2).broadcast_to([P, J, W]),
                                      G.iota_w[:, :].unsqueeze(1).broadcast_to([P, J, W]), ALU.is_equal).then_inc(oh_ok, 1)
                    if update:
                        dve.wait_ge(win_in[q], 16 * (i + 1))
                        if later(t, 4):
                            dve.wait_ge(updated, t - 3)
                        dve.tensor_tensor(winbd[q][:, :, :], win[q][:, :].unsqueeze(1).broadcast_to([P, J, D]),
                                          G.blockmask[:, :, :].broadcast_to([P, J, D]), ALU.mult).then_inc(winbd_ok, 1)

                def add_update(t, q, i):
                    dve.wait_ge(updated, t + 1)
                    dve.wait_ge(rows_in[q], 16 * J * (i + 1))
                    if later(t, 4):
                        dve.wait_ge(new_turned, t - 3)
                    dve.tensor_tensor(new[q][:, :, :], ps_u[q % 2][:, 0:C].rearrange("p (j c) -> p j c", j=J),
                                      rows[q][:, :, 0:D], ALU.add).then_inc(new_pre, 1)

                def add_message(t, q, i):
                    dve.wait_ge(msg_mm, t + 1)
                    dve.wait_ge(rows_in[q], 16 * J * (i + 1))
                    if later(t, 4):
                        dve.wait_ge(summed, t - 3)
                    dve.tensor_tensor(msg[q][:, :, :], ps_m[q % 2][:, 0:C].rearrange("p (j c) -> p j c", j=J),
                                      rows[q][:, :, cols - D:cols], ALU.add).then_inc(msg_pre, 1)

                def add(t, q, i):
                    base = dve.value_load(G.base_i[0:1, bass.ds(t, 1)], min_val=0, max_val=S.N - 1)
                    dve.wait_ge(summed, t + 1)
                    dve.wait_ge(added, t + 1)
                    window = G.acc[0:D, bass.ds(base, W)]
                    dve.tensor_tensor(window, window, ps_w[0:D, 0:W], ALU.add).then_inc(added, 1)
                pipeline(dve, S.T, [(0, build)] + ([(1, add_update)] if update else []) + [(2, add_message), (3, add)])
                dve.wait_ge(added, S.T + 1)

            @block.scalar
            def _(act):
                def evacuate(t, q, i):
                    if edges is not None:
                        act.wait_ge(ea_turned, t + 1)
                    if update:
                        act.wait_ge(oh_turned, t + 1)
                        if later(t, 4):
                            act.wait_ge(updated, t - 3)
                        act.copy(ohT[q][:, :], ps_t[q % 2][:, C:C + P]).then_inc(ohT_ok, 1)
                    if edges is not None:
                        if later(t, 4):
                            act.wait_ge(updated if update else msg_mm, t - 3)
                        act.copy(eaT[q][:, :], ps_t[q % 2][:, 0:C]).then_inc(eaT_ok, 1)

                def relu_new(t, q, i):
                    act.wait_ge(new_pre, t + 1)
                    act.activation(new[q][:, :, :], new[q][:, :, :], ACT.Relu).then_inc(new_ok, 1)

                def evacuate_new(t, q, i):
                    act.wait_ge(new_turned, t + 1)
                    if later(t, 4):
                        act.wait_ge(msg_mm, t - 3)
                        if keep is not None:
                            act.wait_ge(kept[q], 16 * i)
                    act.copy(newT[q][:, :], ps_n[:, 0:C]).then_inc(newT_ok, 1)

                def relu_message(t, q, i):
                    act.wait_ge(msg_pre, t + 1)
                    act.activation(msg[q][:, :, :], msg[q][:, :, :], ACT.Relu).then_inc(msg_ok, 1)
                pipeline(act, S.T, [(0, evacuate)] + ([(1, relu_new), (1, evacuate_new)] if update else []) + [(2, relu_message)])

            @block.tensor
            def _(pe):
                def turn(t, q, i):
                    if update:
                        pe.wait_ge(oh_ok, t + 1)
                        if later(t, 2):
                            pe.wait_ge(ohT_ok, t - 1)
                            if edges is not None:
                                pe.wait_ge(eaT_ok, t - 1)
                        pe.transpose(ps_t[q % 2][:, C:C + P], oh[q][:, :, :].rearrange("p j w -> p (j w)"), G.ident[:, :]).then_inc(oh_turned, 1)
                    if edges is not None:
                        if later(t, 2):
                            pe.wait_ge(eaT_ok, t - 1)
                        last = isinstance(t, int) and t == S.TF
                        a = ea_last if last else ea[q]
                        pe.wait_ge(ea_in[q], 16 * (i + 1) + (16 if last and S.TR % J else 0))
                        pe.transpose(ps_t[q % 2][:, 0:P], half(a, 0), G.ident[:, :])
                        pe.transpose(ps_t[q % 2][:, P:2 * P], half(a, 1), G.ident[:, :]).then_inc(ea_turned, 1)

                def update_edges(t, q, i):
                    pe.wait_ge(ohT_ok, t + 1)
                    pe.wait_ge(winbd_ok, t + 1)
                    wait_eaT(pe, t, q, i)
                    if later(t, 2):
                        pe.wait_ge(new_pre, t - 1)
                    spread = winbd[q][:, :, :].rearrange("p j c -> p (j c)")
                    for k in (0, 1):
                        pe.matmul(half(ps_u[q % 2], k), ohT[q][:, :], spread[:, k * P:(k + 1) * P], start=True, stop=False)
                        ins = pe.matmul(half(ps_u[q % 2], k), half(eaT[q], k), w_edge, start=False, stop=True)
                    ins.then_inc(updated, 1)

                def turn_new(t, q, i):
                    pe.wait_ge(new_ok, t + 1)
                    if later(t, 1):
                        pe.wait_ge(newT_ok, t)
                    a = new[q][:, :, :].rearrange("p j c -> p (j c)")
                    pe.transpose(ps_n[:, 0:P], a[:, 0:P], G.ident[:, :])
                    pe.transpose(ps_n[:, P:2 * P], a[:, P:2 * P], G.ident[:, :]).then_inc(new_turned, 1)

                def messages(t, q, i):
                    if update:
                        pe.wait_ge(newT_ok, t + 1)
                    else:
                        wait_eaT(pe, t, q, i)
                    if later(t, 2):
                        pe.wait_ge(msg_pre, t - 1)
                    pe.matmul(ps_m[q % 2][:, 0:P], half(newT[q], 0), w_msg, start=True, stop=True)
                    pe.matmul(ps_m[q % 2][:, P:2 * P], half(newT[q], 1), w_msg, start=True, stop=True).then_inc(msg_mm, 1)

                def scatter(t, q, i):
                    pe.wait_ge(msg_ok, t + 1)
                    pe.wait_ge(oh_ok, t + 1)
                    if later(t, 1):
                        pe.wait_ge(added, t + 1)
                    for j in range(J):
                        ins = pe.matmul(ps_w[0:D, 0:W], msg[q][:, j, :], oh[q][:, j, :], start=(j == 0), stop=(j == J - 1))
                    ins.then_inc(summed, 1)
                stages = [(0, turn)] if update or edges is not None else []
                stages += [(0, update_edges), (1, turn_new), (1, messages)] if update else [(1, messages)]
                pipeline(pe, S.T, stages + [(2, scatter)])


def node_update_phase(nc, S, G, tag, w_sum, w_self, bias, out):
    with ExitStack() as ctx:
        sb = lambda name, shape, dt: ctx.enter_context(nc.sbuf_tensor(name + tag, shape, dt))
        sem = phase_semaphores(nc, ctx, tag)
        xT = [sb(f"u_xT{u}", [D, P], F32) for u in (0, 1)]
        hid, square = sb("u_hid", [P, S.NB, D], F32), sb("u_square", [P, S.NB, D], F32)
        norm = sb("u_norm", [P, S.NB], F32)
        ps_t = [ctx.enter_context(nc.psum_tensor(f"ps_ut{tag}{u}", [P, 512], F32)) for u in (0, 1)]
        ps_m = [ctx.enter_context(nc.psum_tensor(f"ps_um{tag}{u}", [P, 512], F32)) for u in (0, 1)]
        turned, copied, product, scaled, taken, chain, sq_ok, root_ok = (
            sem("u_" + n) for n in ("turned", "copied", "product", "scaled", "taken", "chain", "sq", "root"))
        with nc.Block() as block:
            @block.tensor
            def _(pe):
                for b in range(S.NB):
                    u = b % 2
                    if b >= 2:
                        pe.wait_ge(copied, b - 1)
                        pe.wait_ge(taken, b - 1)
                    pe.transpose(ps_t[u][0:D, 0:P], G.x[:, b, :], G.ident[:, :]).then_inc(turned, 1)
                    pe.matmul(ps_m[u][:, 0:D], G.acc[0:D, b * P:(b + 1) * P], w_sum, start=True, stop=True)
                    pe.wait_ge(copied, b + 1)
                    pe.matmul(ps_m[u][:, D:2 * D], xT[u][:, :], w_self, start=True, stop=True).then_inc(product, 1)

            @block.scalar
            def _(act):
                for b in range(S.NB):
                    act.wait_ge(turned, b + 1)
                    if b >= 2:
                        act.wait_ge(product, b - 1)
                    act.copy(xT[b % 2][:, :], ps_t[b % 2][0:D, 0:P]).then_inc(copied, 1)
                act.wait_ge(sq_ok, 1)
                act.activation(norm[:, :], norm[:, :], ACT.Sqrt).then_inc(root_ok, 1)

            @block.vector
            def _(dve):
                for b in range(S.NB):
                    dve.wait_ge(product, b + 1)
                    dve.tensor_scalar(hid[:, b, :], ps_m[b % 2][:, 0:D], G.inv_cnt[:, b:b + 1], None, ALU.mult).then_inc(scaled, 1)
                    dve.wait_ge(scaled, b + 1)
                    dve.tensor_tensor(hid[:, b, :], hid[:, b, :], ps_m[b % 2][:, D:2 * D], ALU.add).then_inc(taken, 1)
                dve.wait_ge(taken, S.NB)
                link = Chain(dve, chain)
                link(dve.tensor_tensor(hid[:, :, :], hid[:, :, :], bias.unsqueeze(1).broadcast_to([P, S.NB, D]), ALU.add))
                link(dve.tensor_scalar(hid[:, :, :], hid[:, :, :], 0.0, None, ALU.max))
                link(dve.tensor_tensor(square[:, :, :], hid[:, :, :], hid[:, :, :], ALU.mult))
                link(dve.reduce_sum(norm[:, :], square[:, :, :], axis=AX.X))
                link(dve.tensor_scalar(norm[:, :], norm[:, :], 1e-24, None, ALU.max))
                dve.sem_inc(sq_ok, 1)
                dve.wait_ge(root_ok, 1)
                link(dve.reciprocal(norm[:, :], norm[:, :]))
                link(dve.tensor_tensor(G.x[:, :, :], hid[:, :, :], norm[:, :].unsqueeze(2).broadcast_to([P, S.NB, D]), ALU.mult))
                if out:
                    link(dve.tensor_tensor(G.y[:, :, :], G.x[:, :, :], G.x0[:, :, :], ALU.add))


def store_phase(nc, S, G, out):
    with ExitStack() as ctx:
        out_done = ctx.enter_context(nc.semaphore("out_done"))
        with nc.Block() as block:
            @block.sync
            def _(sp):
                sp.dma_start(out[0:S.NF * P, :].rearrange("(b p) c -> p b c", p=P), G.x[:, 0:S.NF, :]).then_inc(out_done, 16)
                sp.dma_start(out[S.NF * P:S.N, :], G.x[0:S.NR, S.NF, :]).then_inc(out_done, 16)
                sp.wait_ge(out_done, 32)


class Space:
    pass


def gnn_program(nc, x, src, dst, edge_attr_16, edge_attr_64, W_node, W_edge, attn_src, attn_dst, ln_gamma, ln_beta,
                msg_W, msg_b, agg_W, agg_b, edge_W, edge_b, out):
    S = Shapes(x.shape[0], src.shape[0])
    G = Space()
    C0 = D + H
    dram = lambda name, rows, cols: nc.dram_tensor(name, (rows, cols), F32, kind="Internal").ap()
    table0, tableA, max_table = dram("table0", S.NP, C0), dram("table_target", S.NP, H), dram("max_table", S.NP, H)
    gathered = dram("gathered", S.T * P, J * C0)
    msg_table0 = dram("msg_table0", S.NP, D)
    src_table = [dram(f"src_table{l}", S.NP, 2 * D) for l in (1, 2)]
    dst_table = [dram(f"dst_table{l}", S.NP, D) for l in (1, 2)]
    kept = dram("kept_edges", S.T * P, J * D)
    with ExitStack() as ctx:
        sb = lambda name, shape, dt: ctx.enter_context(nc.sbuf_tensor(name, shape, dt))
        G.ident, G.ident_bf = sb("ident", [P, P], F32), sb("ident_bf", [P, P], BF16)
        G.blockmask = sb("blockmask", [P, J, 1], F32)
        G.stack_id = sb("stack_id", [P, W], F32)
        G.iota_w, G.iota_p = sb("iota_w", [P, W], F32), sb("iota_p", [P, P], F16)
        G.ones_bf = sb("ones_bf", [P, 1], BF16)
        G.x, G.y = (sb(n, [P, S.NB, D], F32) for n in ("x", "y"))
        G.src_i, G.base_i = sb("src_i", [P, S.T * J], I32), sb("base_i", [1, S.T], I32)
        G.rel = sb("rel", [P, S.T, J], F32)
        G.inv_cnt = sb("inv_cnt", [P, S.NB], F32)
        G.acc = sb("acc", [C0, S.NP], F32)
        widths = {"w0": D + 2 * H, "w_attn": 2 * H, "w_edge16": J * H, "gamma": D, "beta": D,
                  "table_w0": D, "table_w1": 3 * D, "table_w2": 3 * D, "msg0": P, "msg1": P, "msg2": P, "edge0": P, "edge1": P,
                  "sum0": D, "sum1": D, "sum2": D, "self0": D, "self1": D, "self2": D, "bias0": D, "bias1": D, "bias2": D}
        G.weights = sb("weights", [P, sum(widths.values())], F32)
        at, wt = 0, {}
        for name, width in widths.items():
            wt[name] = G.weights[:, at:at + width]
            at += width
        G.w0, G.w_attn, G.w_edge16, G.gamma, G.beta = (wt[n] for n in ("w0", "w_attn", "w_edge16", "gamma", "beta"))
        flat = lambda a: a.rearrange("(o c) -> o c", o=1)
        everywhere = lambda a: flat(a).broadcast_to([P, D])
        copies = [(G.w0[0:D, 0:D], W_node), (G.gamma, everywhere(ln_gamma)), (G.beta, everywhere(ln_beta))]
        for k, a in enumerate((attn_src, attn_dst)):
            for h in range(H):
                copies.append((G.w_attn[h * HD:(h + 1) * HD, k * H + h:k * H + h + 1], a[h, :].rearrange("(c o) -> c o", o=1)))
        for j in range(J):
            copies.append((G.w_edge16[j * 16:(j + 1) * 16, j * H:(j + 1) * H], W_edge))
        for l in range(3):
            for k in range(2):
                copies.append((wt[f"msg{l}"][k * D:(k + 1) * D, k * D:(k + 1) * D], msg_W[l, D:2 * D, :]))
                if l < 2:
                    copies.append((wt[f"edge{l}"][k * D:(k + 1) * D, k * D:(k + 1) * D], edge_W[l, 2 * D:3 * D, :]))
            copies += [(wt[f"sum{l}"][0:D, :], agg_W[l, 0:D, :]), (wt[f"self{l}"][0:D, :], agg_W[l, D:2 * D, :]),
                       (wt[f"bias{l}"], everywhere(agg_b[l, :]))]
            c = 0 if l == 0 else D
            copies += [(wt[f"table_w{l}"][0:D, c:c + D], msg_W[l, 0:D, :]), (wt[f"table_w{l}"][D:D + 1, c:c + D], flat(msg_b[l, :]))]
            if l:
                copies += [(wt[f"table_w{l}"][0:D, 0:D], edge_W[l - 1, 0:D, :]), (wt[f"table_w{l}"][D:D + 1, 0:D], flat(edge_b[l - 1, :])),
                           (wt[f"table_w{l}"][0:D, 2 * D:3 * D], edge_W[l - 1, D:2 * D, :])]

        G.adj = sb("adj", [P, S.NB, S.NP], mybir.dt.uint8)
        with nc.sbuf_tensor("iota_key", [P, S.NB * W], F16) as G.iota_key, nc.sbuf_tensor("src_r", [P, S.T, J], F32) as G.src_r, \
                nc.sbuf_tensor("key", [P, S.T, J], F32) as G.key:
            setup_phase(nc, S, G, x, src, dst, copies)
            attention_weights_phase(nc, S, G)
            project_phase(nc, S, G, "0", G.w0[0:D + 1, :], D + 2 * H, [(0, C0, table0), (C0, C0 + H, tableA)])
            scores_phase(nc, S, G, table0, tableA, edge_attr_16, gathered, max_table)
        softmax_phase(nc, S, G, max_table, gathered)
        attention_nodes_phase(nc, S, G, table0)
        norm_phase(nc, S, G, "0a", True, G.y)
        norm_phase(nc, S, G, "0b", False, G.x)
        with ExitStack() as own:
            propagate_phase(nc, S, G, "1", G.adj, (1.0, 0.8, 0.5, 0.3), lambda n, s, d: own.enter_context(nc.sbuf_tensor(n, s, d)))
        norm_phase(nc, S, G, "1", False, G.x)
        with nc.sbuf_tensor("x0", [P, S.NB, D], F32) as G.x0:
            keep_x_phase(nc, S, G)
            project_phase(nc, S, G, "A", wt["table_w0"][0:D + 1, 0:D], D, [(0, D, msg_table0)])
            edge_phase(nc, S, G, "A", msg_table0, D, None, None, wt["msg0"], edge_attr_64, None, None)
            node_update_phase(nc, S, G, "A", wt["sum0"][0:D, :], wt["self0"][0:D, :], wt["bias0"], False)
            for l in (1, 2):
                project_phase(nc, S, G, "BC"[l - 1], wt[f"table_w{l}"][0:D + 1, :], 3 * D,
                              [(0, 2 * D, src_table[l - 1]), (2 * D, 3 * D, dst_table[l - 1])])
                edge_phase(nc, S, G, "BC"[l - 1], src_table[l - 1], 2 * D, dst_table[l - 1], wt[f"edge{l - 1}"], wt[f"msg{l}"],
                           edge_attr_64 if l == 1 else None, kept if l == 2 else None, kept if l == 1 else None)
                node_update_phase(nc, S, G, "BC"[l - 1], wt[f"sum{l}"][0:D, :], wt[f"self{l}"][0:D, :], wt[f"bias{l}"], l == 2)
        norm_phase(nc, S, G, "2", False, G.x)
        with nc.sbuf_tensor("adjT", [P, S.NB, S.NP], mybir.dt.uint8) as adjT:
            transpose_counts_phase(nc, S, G, G.adj, adjT)
            taken = [0]

            def in_adj(name, shape, dt):
                size = shape[1] * (shape[2] if len(shape) > 2 else 1) * (4 if dt == F32 else 2)
                at0, taken[0] = taken[0], taken[0] + -(-size // 32) * 32
                a = G.adj[:, :, :].rearrange("p b n -> p (b n)")[:, at0:at0 + size].bitcast(dt)
                return a.rearrange("p (b c) -> p b c", c=shape[2]) if len(shape) > 2 else a
            propagate_phase(nc, S, G, "3", adjT, None, in_adj)
        norm_phase(nc, S, G, "3", False, G.x)
        store_phase(nc, S, G, out)


def keep_x_phase(nc, S, G):
    with nc.semaphore("kept_x") as done, nc.Block() as block:
        @block.vector
        def _(dve):
            dve.tensor_copy(G.x0[:, :, :], G.x[:, :, :]).then_inc(done, 1)
            dve.wait_ge(done, 1)


_INS = ['x', 'src', 'dst', 'edge_attr_16', 'edge_attr_64', 'L0_gnn_W_node', 'L0_gnn_W_edge', 'L0_gnn_attn_src', 'L0_gnn_attn_dst',
        'L0_gnn_ln_gamma', 'L0_gnn_ln_beta', 'L2_gnn_msg_W', 'L2_gnn_msg_b', 'L2_gnn_agg_W', 'L2_gnn_agg_b', 'L2_gnn_edge_W', 'L2_gnn_edge_b']


def kernel(**inputs):
    import numpy as _np
    import concourse.bacc as _bacc
    from concourse import mybir as _mybir
    from concourse.bass_utils import run_bass_kernel_spmd as _run

    nc = _bacc.Bacc("TRN2", target_bir_lowering=False, num_devices=1)
    arrays, args = {}, []
    for name in _INS:
        a = _np.ascontiguousarray(inputs[name])
        arrays[f"in_{name}_dram"] = a
        args.append(nc.dram_tensor(f"in_{name}_dram", a.shape, _mybir.dt.from_np(a.dtype), kind="ExternalInput").ap())
    args.append(nc.dram_tensor("out_0_dram", inputs["x"].shape, _mybir.dt.float32, kind="ExternalOutput").ap())
    gnn_program(nc, *args)
    r = _run(nc, [arrays], core_ids=[0])
    return r.results[0]["out_0_dram"]
```

```python
import concourse.bass as bass
from concourse import mybir
from contextlib import ExitStack

F32, BF16, F16, I32 = mybir.dt.float32, mybir.dt.bfloat16, mybir.dt.float16, mybir.dt.int32
ALU = mybir.AluOpType
ACT = mybir.ActivationFunctionType
AX = mybir.AxisListType
P = 128
J = 4
CH = P * J
W = 24
JW = J * W
LAG = 2
D = 64
H = 4
HD = D // H


class Shapes:

    def __init__(self, n, e):
        self.N, self.E = n, e
        self.NB = -(-(n + W - 1) // P)
        self.NP = self.NB * P
        self.NF = n // P
        self.NR = n - self.NF * P
        self.T = -(-e // CH)
        self.TF = e // CH
        self.TR = e - self.TF * CH
        self.NW = -(-n // W)
        assert self.T == self.TF + 1 and self.TR > 0 and self.T <= 512 and W >= H


def later(t, ring):
    return not (isinstance(t, int) and t < ring)


def pipeline(eng, n, stages, ring=4, windows=None):
    def turn(i, q0):
        if windows and q0 == 0:
            windows.load(i)
        for lag, step in stages:
            q, borrow = (q0 - lag) % ring, (q0 - lag) // ring
            if windows:
                windows.place = ring * (1 + borrow) + q
            if isinstance(i, int):
                t = ring * i + q0 - lag
                if 0 <= t < n:
                    step(t, q, t // ring)
            else:
                step(ring * i + (q0 - lag), q, i + borrow)

    last = (n - 1) // ring
    for t in range(2 * ring):
        turn(t // ring, t % ring)
    with eng.Fori(2, last) as i:
        for q0 in range(ring):
            turn(i, q0)
    for t in range(ring * last, n + max(lag for lag, _ in stages)):
        turn(t // ring, t % ring)


class WindowBases:

    def __init__(self, nc, eng_type, S, G, ring):
        self.nc, self.eng_type, self.S, self.G, self.ring = nc, eng_type, S, G, ring
        self.place = 0

    def load(self, i):
        first, count = self.ring * (i - 1), 2 * self.ring
        if isinstance(i, int):
            start, stop = max(first, 0), min(first + count, self.S.T)
            cells, missing = self.G.base_cur[0:1, start:stop], start - first
        else:
            cells, missing = self.G.base_cur[0:1, bass.ds(first, count)], 0
        _, values = self.nc.values_load_multi_w_load_instructions(cells, engines=[self.eng_type], min_val=0, max_val=self.S.NP - W,
                                                                    skip_runtime_bounds_check_because="a base is a node's number")
        self.values = [None] * missing + list(values)

    def base(self):
        return self.values[self.place]


def blocks(eng, n, step):
    for u in (0, 1):
        step(u, u, 0)
    if n // 2 > 1:
        with eng.Fori(1, n // 2) as i:
            for u in (0, 1):
                step(2 * i + u, u, i)
    if n % 2:
        step(n - 1, 0, n // 2)


class Chain:

    def __init__(self, eng, sem):
        self.eng, self.sem, self.n = eng, sem, 0

    def __call__(self, ins):
        self.n += 1
        ins.then_inc(self.sem, 1)
        self.eng.wait_ge(self.sem, self.n)


def phase_semaphores(nc, ctx, tag=""):
    taken = []

    def sem(name):
        taken.append(nc.alloc_semaphore(name=name + tag))
        return taken[-1]

    def close():
        nc.clear_and_free_semaphores(taken)
        nc.all_engine_barrier()
    ctx.callback(close)
    return sem


def node_view(dram, s):
    return dram.rearrange("(b p) c -> p b c", p=P)


def setup_phase(nc, S, G, x, src, dst, copies):
    TB = -(-S.T // P)
    with ExitStack() as ctx:
        sb = lambda name, shape, dt: ctx.enter_context(nc.sbuf_tensor(name, shape, dt))
        sem = phase_semaphores(nc, ctx)
        rows_i = sb("rows_i", [P, 2, TB, CH], I32)
        rows_f = sb("rows_f", [P, 2, TB, CH], F32)
        inside, below = sb("inside", [P, TB, CH], F32), sb("below", [P, TB, CH], F32)
        base_col, top_col, count_col = sb("base_col", [P, TB], F32), sb("top_col", [P, TB], F32), sb("count_col", [P, 1], F32)
        ones_col, ones_row = sb("ones_col", [P, 1], F32), sb("ones_row", [1, P], F32)
        base_row, top_row, cmp_row, flags = (sb(n, [1, c], F32) for n, c in
                                             (("base_row", S.T), ("top_row", TB * P), ("cmp_row", S.T), ("flags", 8)))
        src_f, dst_f = sb("src_f", [P, S.T, J], F32), sb("dst_f", [P, S.T, J], F32)
        blk_i, tmp = sb("blk_i", [P, S.T, J], I32), sb("tmp", [P, S.T, J], F32)
        ps = [ctx.enter_context(nc.psum_tensor(f"ps_set{i}", [P, 512], F32)) for i in range(2)]
        ps_top, ps_count, ps_base = (ctx.enter_context(nc.psum_tensor(n, [P, 512], F32)) for n in ("ps_top", "ps_count", "ps_base"))
        idx_clear, idx_in, x_in, x_clear, rows_ready, w_clear, w_in = (
            sem(n) for n in ("idx_clear", "idx_in", "x_in", "x_clear", "rows_ready", "w_clear", "w_in"))
        ident_z, ident_ok, iotas, turned, moved, vch, cols_ok, topped, base_ok, spread = (
            sem(n) for n in ("ident_z", "ident_ok", "iotas", "turned", "moved", "vch", "cols_ok", "topped", "base_ok", "spread"))
        last = S.TF - (TB - 1) * P
        with nc.Block() as block:
            @block.sync
            def _(sp):
                sp.wait_ge(idx_clear, 3)
                for k, a in enumerate((src, dst)):
                    for b in range(TB):
                        rows = min(P, S.TF - b * P)
                        sp.dma_start(rows_i[0:rows, k, b, :],
                                     a[b * P * CH:(b * P + rows) * CH].rearrange("(t e) -> t e", e=CH)).then_inc(idx_in, 16)
                    sp.dma_start(rows_i[last:last + 1, k, TB - 1, 0:S.TR],
                                 a[S.TF * CH:S.E].rearrange("(t e) -> t e", t=1)).then_inc(idx_in, 16)
                sp.dma_start(G.base_i[0:1, 0:S.TF],
                             dst[0:S.TF * CH].rearrange("(o t e) -> o t e", o=1, e=CH)[:, :, 0], allow_slow_non_contiguous=True).then_inc(idx_in, 16)
                sp.dma_start(G.base_i[0:1, S.TF:S.T], dst[S.TF * CH:S.TF * CH + 1].rearrange("(t e) -> t e", t=1)).then_inc(idx_in, 16)
                sp.wait_ge(x_clear, 1)
                sp.dma_start(G.x[:, 0:S.NF, :], x[0:S.NF * P, :].rearrange("(b p) c -> p b c", p=P)).then_inc(x_in, 16)
                sp.dma_start(G.x[0:S.NR, S.NF, :], x[S.NF * P:S.N, :]).then_inc(x_in, 16)
                sp.wait_ge(x_in, 32)

            @block.gpsimd
            def _(pool):
                pool.memset(G.ident[:, :], 0.0).then_inc(ident_z, 1)
                pool.memset(G.blockmask[:, :, :], 1.0).then_inc(ident_z, 1)
                pool.memset(G.stack_id[:, :], 0.0).then_inc(ident_z, 1)
                pool.iota(G.iota_w[:, :], [[1, W]], base=0, channel_multiplier=0, allow_small_or_imprecise_dtypes=True).then_inc(iotas, 1)
                pool.iota(G.iota_p[:, :], [[1, P]], base=0, channel_multiplier=0, allow_small_or_imprecise_dtypes=True).then_inc(iotas, 1)
                pool.iota(G.iota_key[:, :], [[1, S.NB * W]], base=0, channel_multiplier=0, allow_small_or_imprecise_dtypes=True).then_inc(iotas, 1)
                pool.wait_ge(ident_z, 3)
                pool.affine_select(out=G.ident[:, :], in_=G.ident[:, :], compare_op=ALU.not_equal, fill=1.0, base=0,
                                   pattern=[[-1, P]], channel_multiplier=1).then_inc(ident_ok, 1)
                pool.affine_select(out=G.blockmask[:, :, 0], in_=G.blockmask[:, :, 0], compare_op=ALU.is_ge, fill=0.0, base=0,
                                   pattern=[[-W, J]], channel_multiplier=1).then_inc(ident_ok, 1)
                pool.wait_ge(ident_ok, 2)
                pool.affine_select(out=G.blockmask[:, :, 0], in_=G.blockmask[:, :, 0], compare_op=ALU.is_ge, fill=0.0, base=W - 1,
                                   pattern=[[W, J]], channel_multiplier=-1).then_inc(ident_ok, 1)
                for j in range(J):
                    pool.wait_ge(ident_ok, 3 + j)
                    pool.affine_select(out=G.stack_id[:, :], in_=G.stack_id[:, :], compare_op=ALU.not_equal, fill=1.0, base=-j * W,
                                       pattern=[[-1, W]], channel_multiplier=1).then_inc(ident_ok, 1)
                pool.wait_ge(ident_ok, 3 + J)
                pool.wait_ge(iotas, 3)

            @block.vector
            def _(dve):
                dve.memset(rows_i[:, 0, :, :], 0).then_inc(idx_clear, 1)
                dve.memset(rows_i[:, 1, :, :], -1).then_inc(idx_clear, 1)
                dve.memset(top_col[:, :], 0.0).then_inc(idx_clear, 1)
                dve.memset(G.x[:, :, :], 0.0).then_inc(x_clear, 1)
                dve.memset(G.weights[:, :], 0.0).then_inc(w_clear, 1)
                link = Chain(dve, vch)
                link(dve.memset(ones_col[:, :], 1.0))
                link(dve.memset(ones_row[:, :], 1.0))
                link(dve.memset(G.ones_bf[:, :], 1.0))
                dve.wait_ge(idx_in, 16 * (2 * (TB + 1) + 2))
                link(dve.tensor_copy(rows_f[:, :, :, :], rows_i[:, :, :, :]))
                dve.sem_inc(rows_ready, 1)
                link(dve.tensor_copy(base_col[:, :], rows_f[:, 1, :, 0]))
                link(dve.reduce_max(top_col[:, :], rows_f[:, 1, :, :], axis=AX.X))
                for b in range(TB):
                    link(dve.tensor_scalar(inside[:, b, :], rows_f[:, 1, b, :], base_col[:, b:b + 1], 0.0, ALU.subtract, ALU.is_ge))
                    link(dve.tensor_scalar(below[:, b, :], rows_f[:, 1, b, :], base_col[:, b:b + 1], float(W), ALU.subtract, ALU.is_lt))
                link(dve.tensor_tensor(inside[:, :, :], inside[:, :, :], below[:, :, :], ALU.mult))
                link(dve.tensor_scalar(below[:, :, :], rows_f[:, 1, :, :], 0.0, None, ALU.is_ge))
                link(dve.tensor_tensor(inside[:, :, :], inside[:, :, :], below[:, :, :], ALU.mult))
                link(dve.reduce_sum(count_col[:, :], inside[:, :, :].rearrange("p b e -> p (b e)"), axis=AX.X))
                dve.sem_inc(cols_ok, 1)
                dve.wait_ge(topped, 1)
                link(dve.tensor_copy(top_row[:, :], ps_top[0:1, 0:TB * P]))
                link(dve.tensor_copy(base_row[:, :], G.base_i[:, :]))
                link(dve.tensor_scalar(flags[:, 0:1], ps_count[0:1, 0:1], float(S.E), None, ALU.is_equal))
                link(dve.tensor_tensor(cmp_row[:, 0:S.T - 1], base_row[:, 1:S.T], base_row[:, 0:S.T - 1], ALU.is_ge))
                link(dve.reduce_sum(flags[:, 1:2], cmp_row[:, 0:S.T - 1], axis=AX.X))
                link(dve.tensor_tensor(cmp_row[:, 0:S.T - LAG], base_row[:, LAG:S.T], top_row[:, 0:S.T - LAG], ALU.is_gt))
                link(dve.reduce_sum(flags[:, 2:3], cmp_row[:, 0:S.T - LAG], axis=AX.X))
                link(dve.tensor_scalar(flags[:, 1:2], flags[:, 1:2], float(S.T - 1), None, ALU.is_equal))
                link(dve.tensor_scalar(flags[:, 2:3], flags[:, 2:3], float(S.T - LAG), None, ALU.is_equal))
                link(dve.tensor_tensor(flags[:, 1:2], flags[:, 1:2], flags[:, 2:3], ALU.mult))
                link(dve.tensor_tensor(flags[:, 1:2], flags[:, 1:2], flags[:, 0:1], ALU.mult))
                link(dve.tensor_scalar(flags[:, 3:4], flags[:, 0:1], -float(S.NW - 1), float(S.NW), ALU.mult, ALU.add))
                link(dve.tensor_scalar(flags[:, 4:5], flags[:, 1:2], -1.0, 2.0, ALU.mult, ALU.add))
                link(dve.tensor_copy(G.control[:, 0:2], flags[:, 3:5]))
                link(dve.tensor_scalar(base_row[:, :], base_row[:, :], flags[:, 0:1], None, ALU.mult))
                link(dve.tensor_copy(G.base_i[:, :], base_row[:, :]))
                dve.sem_inc(base_ok, 1)
                n = 0
                for k, out in enumerate((src_f, dst_f)):
                    for b in range(TB):
                        rows = min(P, S.T - b * P)
                        for j in range(J):
                            dve.wait_ge(turned, n + 1)
                            dve.tensor_copy(out[:, b * P:b * P + rows, j], ps[n % 2][:, 0:rows]).then_inc(moved, 1)
                            n += 1
                dve.wait_ge(moved, n)
                flat = lambda a: a[:, :, :].rearrange("p t j -> p (t j)")
                link(dve.tensor_copy(G.src_i[:, :], flat(src_f)))
                link(dve.tensor_scalar(tmp[:, :, :], dst_f[:, :, :], 0.0, None, ALU.max))
                link(dve.tensor_copy(G.dst_i[:, :], flat(tmp)))
                link(dve.tensor_scalar(G.real[:, :], flat(dst_f), 0.0, None, ALU.is_ge))
                dve.wait_ge(spread, 1)
                link(dve.tensor_tensor(G.rel[:, :, :], dst_f[:, :, :], ps_base[:, 0:S.T].unsqueeze(2).broadcast_to([P, S.T, J]), ALU.subtract))
                link(dve.tensor_scalar(blk_i[:, :, :], G.src_i[:, :].rearrange("p (t j) -> p t j", j=J), 7, None, ALU.arith_shift_right))
                link(dve.tensor_copy(G.src_b[:, :, :], blk_i[:, :, :]))
                link(dve.tensor_scalar(tmp[:, :, :], G.src_b[:, :, :], -float(P), None, ALU.mult))
                link(dve.tensor_tensor(G.src_r[:, :, :], src_f[:, :, :], tmp[:, :, :], ALU.add))
                link(dve.tensor_scalar(G.src_neg[:, :, :], G.src_r[:, :, :], -1.0, None, ALU.mult))
                dve.wait_ge(ident_ok, 1)
                link(dve.tensor_copy(G.ident_bf[:, :], G.ident[:, :]))

            @block.scalar
            def _(act):
                act.wait_ge(w_clear, 1)
                for dst_ap, src_ap in copies:
                    act.dma_start(dst_ap, src_ap).then_inc(w_in, 16)
                act.wait_ge(w_in, 16 * len(copies))

            @block.tensor
            def _(pe):
                pe.wait_ge(ident_ok, 1)
                pe.wait_ge(cols_ok, 1)
                pe.wait_ge(vch, 2)
                for b in range(TB):
                    pe.matmul(ps_top[0:1, b * P:(b + 1) * P], top_col[:, b:b + 1], G.ident[:, :], start=True, stop=True)
                pe.matmul(ps_count[0:1, 0:1], count_col[:, :], ones_col[:, :], start=True, stop=True).then_inc(topped, 1)
                pe.wait_ge(base_ok, 1)
                pe.matmul(ps_base[:, 0:S.T], ones_row[:, :], base_row[:, :], start=True, stop=True).then_inc(spread, 1)
                pe.wait_ge(rows_ready, 1)
                n = 0
                for k in range(2):
                    for b in range(TB):
                        rows = min(P, S.T - b * P)
                        for j in range(J):
                            if n >= 2:
                                pe.wait_ge(moved, n - 1)
                            pe.transpose(ps[n % 2][:, 0:rows],
                                         rows_f[0:rows, k, b, :].rearrange("t (p j) -> t p j", j=J)[:, :, j],
                                         G.ident[0:rows, 0:rows]).then_inc(turned, 1)
                            n += 1


def first_window_phase(nc, S, G, tag, tiles):
    with ExitStack() as ctx:
        done = phase_semaphores(nc, ctx, tag)("first_window")
        with nc.Block() as block:
            @block.vector
            def _(dve):
                dve.tensor_copy(G.window[:, :], G.iota_w[:, :]).then_inc(done, 1)
                dve.tensor_copy(G.base_cur[:, :], G.base_i[:, :]).then_inc(done, 1)
                for a in tiles:
                    dve.memset(a, 0.0).then_inc(done, 1)
                dve.wait_ge(done, 2 + len(tiles))


def next_window(dve, G, done):
    dve.tensor_scalar(G.window[:, :], G.window[:, :], float(W), None, ALU.add).then_inc(done, 1)
    dve.tensor_scalar(G.base_cur[:, :], G.base_cur[:, :], float(W), None, ALU.add).then_inc(done, 1)
    dve.wait_ge(done, 2)


def project_phase(nc, S, G, tag, wcat, wcols, outs):
    with ExitStack() as ctx:
        sb = lambda name, shape, dt: ctx.enter_context(nc.sbuf_tensor(name, shape, dt))
        sem = phase_semaphores(nc, ctx)
        staged = [sb(f"staged{tag}{u}", [P, D], F32) for u in (0, 1)]
        xT = [sb(f"xT{tag}{u}", [D + 1, P], F32) for u in (0, 1)]
        table = sb(f"tab{tag}", [P, S.NB, wcols], F32)
        ps_t = [ctx.enter_context(nc.psum_tensor(f"ps_t{tag}{u}", [P, 512], F32)) for u in (0, 1)]
        ps_m = [ctx.enter_context(nc.psum_tensor(f"ps_m{tag}{u}", [P, 512], F32)) for u in (0, 1)]
        st, tr, ev, mm, tb, out_done, ones, begun = (sem(n + tag) for n in ("st", "tr", "ev", "mm", "tb", "tab_out", "ones", "begun"))
        with nc.Block() as block:
            @block.sync
            def _(sp):
                sp.wait_ge(tb, S.NB)
                for c0, c1, dram in outs:
                    sp.dma_start(node_view(dram, S), table[:, :, c0:c1]).then_inc(out_done, 16)
                sp.wait_ge(out_done, 16 * len(outs))

            @block.gpsimd
            def _(pool):
                def stage(b, u, i):
                    if not (isinstance(i, int) and i == 0):
                        pool.wait_ge(tr, b - 1)
                    pool.tensor_copy(staged[u][:, :], G.x[:, bass.ds(b, 1), :].rearrange("p o c -> p (o c)")).then_inc(st, 1)
                blocks(pool, S.NB, stage)

            @block.tensor
            def _(pe):
                pe.wait_ge(ones, 2)

                def multiply(b, u):
                    if later(b, 2):
                        pe.wait_ge(tb, b - 1)
                    pe.wait_ge(ev, b + 1)
                    pe.matmul(ps_m[u][:, 0:wcols], xT[u][:, :], wcat, start=True, stop=True).then_inc(mm, 1)

                def project(b, u, i):
                    pe.wait_ge(st, b + 1)
                    if later(b, 2):
                        pe.wait_ge(ev, b - 1)
                    pe.sem_inc(begun, 1)
                    pe.transpose(ps_t[u][0:D, 0:P], staged[u][:, :], G.ident[:, :]).then_inc(tr, 1)
                    if later(b, 1):
                        multiply(b - 1, 1 - u)
                blocks(pe, S.NB, project)
                multiply(S.NB - 1, (S.NB - 1) % 2)

            @block.scalar
            def _(act):
                def evacuate(b, u, i):
                    act.wait_ge(tr, b + 1)
                    if not (isinstance(i, int) and i == 0):
                        act.wait_ge(mm, b - 1)
                    act.copy(xT[u][0:D, :], ps_t[u][0:D, 0:P]).then_inc(ev, 1)
                blocks(act, S.NB, evacuate)

            @block.vector
            def _(dve):
                for u in (0, 1):
                    dve.memset(xT[u][D:D + 1, :], 1.0).then_inc(ones, 1)

                def keep(b, u, i):
                    dve.wait_ge(mm, b + 1)
                    dve.tensor_copy(table[:, bass.ds(b, 1), :].rearrange("p o c -> p (o c)"), ps_m[u][:, 0:wcols]).then_inc(tb, 1)
                blocks(dve, S.NB, keep)


def attention_weights_phase(nc, S, G):
    with ExitStack() as ctx:
        sem = phase_semaphores(nc, ctx)
        wT = ctx.enter_context(nc.sbuf_tensor("wT", [D, D], F32))
        ps = ctx.enter_context(nc.psum_tensor("ps_aw", [P, 512], F32))
        aw_turned, aw_copied, aw_product, aw_done = sem("aw_turned"), sem("aw_copied"), sem("aw_product"), sem("aw_done")
        with nc.Block() as block:
            @block.tensor
            def _(pe):
                pe.transpose(ps[0:D, 0:D], G.w0[0:D, 0:D], G.ident[0:D, 0:D]).then_inc(aw_turned, 1)
                pe.wait_ge(aw_copied, 1)
                pe.matmul(ps[0:D, D:D + 2 * H], wT[:, :], G.w_attn[0:D, :], start=True, stop=True).then_inc(aw_product, 1)

            @block.vector
            def _(dve):
                dve.wait_ge(aw_turned, 1)
                dve.tensor_copy(wT[:, :], ps[0:D, 0:D]).then_inc(aw_copied, 1)
                dve.wait_ge(aw_product, 1)
                dve.tensor_copy(G.w0[0:D, D:D + 2 * H], ps[0:D, D:D + 2 * H]).then_inc(aw_done, 1)
                dve.wait_ge(aw_done, 1)


def window_copy(table, base):
    rows = table[bass.ds(base, W), :]
    return bass.AP(rows.tensor, rows.offset, [[0, J]] + [list(a) for a in rows.ap])


def window_base(eng, S, G, t):
    return eng.value_load(G.base_cur[0:1, bass.ds(t, 1)], min_val=0, max_val=S.NP - W)


def one_hot(dve, S, G, out, t):
    return dve.tensor_tensor(out, G.rel[:, bass.ds(t, 1), :].rearrange("p o j -> p (o j)").unsqueeze(2).broadcast_to([P, J, W]),
                             G.window[:, :].unsqueeze(1).broadcast_to([P, J, W]), ALU.is_equal)


def load_edges(sp, S, tile, last_tile, edges, t, landed):
    if isinstance(t, int) and t == S.TF:
        full, rest, e0, c = S.TR // J, S.TR % J, S.TF * CH, edges.shape[1]
        sp.dma_start(last_tile[0:full, :], edges[e0:e0 + full * J, :].rearrange("(p j) c -> p (j c)", j=J)).then_inc(landed, 16)
        if rest:
            sp.dma_start(last_tile[full:full + 1, 0:rest * c],
                         edges[e0 + full * J:S.E, :].rearrange("(p j) c -> p (j c)", p=1)).then_inc(landed, 16)
    else:
        sp.dma_start(tile[:, :], edges[bass.ds(t * CH, CH), :].rearrange("(p j) c -> p (j c)", j=J)).then_inc(landed, 16)


def edges_landed(S, t, i):
    return 16 * (i + 1) + (16 if isinstance(t, int) and t == S.TF and S.TR % J else 0)


def attention_phase(nc, S, G, table0, tableA, edge_attr_16):
    C0 = D + H
    R = 10
    HALF = S.NB * W // 2
    with ExitStack() as ctx:
        sb = lambda name, shape, dt: ctx.enter_context(nc.sbuf_tensor(name, shape, dt))
        pb = lambda name, cols=512: ctx.enter_context(nc.psum_tensor(name, [P, cols], F32))
        sem = phase_semaphores(nc, ctx)
        ring = lambda f: [f(q) for q in range(R)]
        pair = lambda f: [f(q) for q in range(2)] * (R // 2)
        ea = ring(lambda q: sb(f"s_ea{q}", [P, J * 16], F32))
        ea_last = sb("s_ea_last", [P, J * 16], F32)
        index = ring(lambda q: sb(f"s_index{q}", [P, J], I32))
        win = ring(lambda q: sb(f"s_win{q}", [JW, H], F32))
        rows = ring(lambda q: sb(f"s_rows{q}", [P, J, C0], F32))
        oh = ring(lambda q: sb(f"s_oh{q}", [P, J, W], F32))
        ohT = ring(lambda q: sb(f"s_ohT{q}", [JW, P], F32))
        eaT = pair(lambda q: sb(f"s_eaT{q}", [J * 16, P], F32))
        winbd = pair(lambda q: sb(f"s_winbd{q}", [JW, J, H], F32))
        masked = pair(lambda q: sb(f"s_masked{q}", [P, J, H, W], F32))
        score = pair(lambda q: sb(f"s_score{q}", [P, J, H], F32))
        mcol = pair(lambda q: sb(f"s_mcol{q}", [H * W, 1], F32))
        mdiag = pair(lambda q: sb(f"s_mdiag{q}", [H * W, W], F32))
        mrep = pair(lambda q: sb(f"s_mrep{q}", [H, J, W], F32))
        mbd = pair(lambda q: sb(f"s_mbd{q}", [JW, J, H], F32))
        arg = pair(lambda q: sb(f"s_arg{q}", [P, J, H], F32))
        msg = pair(lambda q: sb(f"s_msg{q}", [P, J, C0], F32))
        away = pair(lambda q: sb(f"s_away{q}", [P, J, P], F16))
        ohsrc = pair(lambda q: sb(f"s_ohsrc{q}", [P, J, P], F16))
        ohkey = pair(lambda q: [sb(f"s_ohkey{q}_{j}", [P, S.NB * W], F16) for j in range(J)])
        key, tmp, valid = (sb(n, [P, S.T, J], F32) for n in ("s_key", "s_tmp", "s_valid"))
        ps_t, ps_s, ps_m, ps_x, ps_e, ps_w = (pb("ps_" + n) for n in ("turned", "scores", "masked", "maxima", "spread", "sums"))
        ps_a = pb("ps_counts", 1024)
        ea_in, win_in, rows_in = (ring(lambda q: sem(f"s_{n}{q}")) for n in ("ea", "wi", "ri"))
        index_ok, indexing, gathering, oh_ok, key_ok, src_ok, winbd_ok, turned, evac, scored, score_ok, attn_ok, masked_ok = (
            sem("s_" + n) for n in ("index", "indexing", "gathering", "oh", "key", "src", "wbd", "turned", "evac", "scored", "score", "attn", "masked"))
        mask_turned, mcol_ok, mdiag_ok, maxima, merged, adj_mm, adj_ok, cleared, vch = (
            sem("s_" + n) for n in ("mturned", "mcol", "mdiag", "maxima", "merged", "adjmm", "adjok", "cleared", "vch"))
        mrep_ok, mspread, mbd_ok, spread, diff_ok, arg_ok, exp_ok, msg_ok, summed, added, away_ok, moved_on, taking, apart = (
            sem("s_" + n) for n in ("mrep", "mspread", "mbd", "spread", "diff", "arg", "exp", "msg", "summed", "added", "away", "moved_on", "taking", "apart"))
        with nc.Block() as block:
            @block.sync
            def _(sp):
                def load(t, q, i):
                    if later(t, R):
                        sp.wait_ge(turned, 2 * (t - R + 1))
                        sp.wait_ge(winbd_ok, t - R + 1)
                    elif isinstance(t, int) and t == 0:
                        sp.wait_ge(cleared, 1)
                    load_edges(sp, S, ea[q], ea_last, edge_attr_16, t, ea_in[q])
                    sp.dma_start(win[q][:, :], window_copy(tableA, window_base(sp, S, G, t))).then_inc(win_in[q], 16)
                pipeline(sp, S.T, [(0, load)], R)

            @block.gpsimd
            def _(pool):
                pool.memset(ea_last[:, :], 0.0).then_inc(cleared, 1)

                def gather(t, q, i):
                    pool.wait_ge(index_ok, t + 1)
                    if later(t, R):
                        pool.wait_ge(msg_ok, t - R + 1)
                        pool.wait_ge(masked_ok, t - R + 1)
                    pool.sem_inc(gathering, 1)
                    for j in range(J):
                        pool.indirect_dma_start(rows[q][:, j, :], None, table0, bass.IndirectOffsetOnAxis(
                            ap=index[q][:, j:j + 1], axis=0)).then_inc(rows_in[q], 16)
                pipeline(pool, S.T, [(0, gather)], R)

            @block.vector
            def _(dve):
                link = Chain(dve, vch)
                link(dve.tensor_scalar(key[:, :, :], G.rel[:, :, :], G.window[:, 0:1], None, ALU.subtract))
                link(dve.tensor_scalar(valid[:, :, :], key[:, :, :], 0.0, None, ALU.is_ge))
                link(dve.tensor_scalar(tmp[:, :, :], key[:, :, :], float(W), None, ALU.is_lt))
                link(dve.tensor_tensor(valid[:, :, :], valid[:, :, :], tmp[:, :, :], ALU.mult))
                link(dve.tensor_scalar(key[:, :, :], key[:, :, :], float(S.NB), 1.0, ALU.mult, ALU.add))
                link(dve.tensor_tensor(key[:, :, :], G.src_b[:, :, :], key[:, :, :], ALU.add))
                link(dve.tensor_tensor(key[:, :, :], key[:, :, :], valid[:, :, :], ALU.mult))
                link(dve.tensor_scalar(key[:, :, :], key[:, :, :], -1.0, None, ALU.add))

                def build(t, q, i):
                    one_hot(dve, S, G, oh[q][:, :, :], t).then_inc(oh_ok, 1)
                    dve.wait_ge(win_in[q], 16 * (i + 1))
                    dve.tensor_tensor(winbd[q][:, :, :], win[q][:, :].unsqueeze(1).broadcast_to([JW, J, H]),
                                      G.blockmask[0:JW, :, :].broadcast_to([JW, J, H]), ALU.mult).then_inc(winbd_ok, 1)
                    for j in range(J):
                        ins = dve.tensor_scalar(ohkey[q][j][:, :], G.iota_key[:, :], key[:, bass.ds(t, 1), j], None, ALU.is_equal)
                    ins.then_inc(key_ok, 1)

                def attend(t, q, i):
                    dve.wait_ge(rows_in[q], 16 * J * (i + 1))
                    dve.wait_ge(scored, t + 1)
                    dve.tensor_tensor(score[q][:, :, :], ps_s[:, 0:J * H].rearrange("p (j h) -> p j h", h=H),
                                      rows[q][:, :, D:C0], ALU.add).then_inc(score_ok, 1)
                    dve.wait_ge(score_ok, t + 1)
                    dve.scalar_tensor_tensor(rows[q][:, :, D:C0], score[q][:, :, :], 0.2, score[q][:, :, :], ALU.mult, ALU.max).then_inc(attn_ok, 1)
                    dve.wait_ge(attn_ok, t + 1)
                    dve.tensor_tensor(masked[q][:, :, :, :], rows[q][:, :, D:C0].unsqueeze(3).broadcast_to([P, J, H, W]),
                                      oh[q][:, :, :].unsqueeze(2).broadcast_to([P, J, H, W]), ALU.mult).then_inc(masked_ok, 1)

                def add_counts(t, q, i):
                    window = G.adj[:, :, bass.ds(windows.base(), W)]
                    dve.wait_ge(adj_ok, t) if later(t, 1) else None
                    dve.wait_ge(adj_mm, t + 1)
                    window = window.rearrange("p b (k w) -> p k w b", k=2)
                    counts = ps_a[:, :].rearrange("p (k c) -> p k c", k=2)[:, :, 0:HALF].rearrange("p k (w b) -> p k w b", b=S.NB)
                    dve.tensor_tensor(window, window, counts, ALU.add).then_inc(adj_ok, 1)

                def reduce(t, q, i):
                    dve.wait_ge(mask_turned, t + 1)
                    dve.reduce_max(mcol[q][:, :], ps_m[0:H * W, :], axis=AX.X).then_inc(mcol_ok, 1)
                    dve.wait_ge(mcol_ok, t + 1)
                    dve.tensor_scalar(mdiag[q][:, :], G.stack_id[0:H * W, :], mcol[q][:, 0:1], None, ALU.mult).then_inc(mdiag_ok, 1)

                def merge(t, q, i):
                    window = G.maxima[:, bass.ds(windows.base(), W)]
                    if isinstance(t, int) and t == 1:
                        dve.wait_ge(merged, 1)
                    dve.wait_ge(maxima, t + 1)
                    dve.tensor_tensor(window, window, ps_x[0:H, 0:W], ALU.max).then_inc(merged, 1)

                def take_maxima(t, q, i):
                    window = G.maxima[:, bass.ds(windows.base(), W)]
                    dve.wait_ge(merged, min(t + LAG, S.T) if isinstance(t, int) else t + LAG)
                    dve.sem_inc(taking, 1)
                    dve.tensor_copy(mrep[q][:, :, :], window.unsqueeze(1).broadcast_to([H, J, W])).then_inc(mrep_ok, 1)

                def mask_maxima(t, q, i):
                    dve.wait_ge(mspread, t + 1)
                    dve.tensor_tensor(mbd[q][:, :, :], ps_x[0:JW, W:W + H].unsqueeze(1).broadcast_to([JW, J, H]),
                                      G.blockmask[0:JW, :, :].broadcast_to([JW, J, H]), ALU.mult).then_inc(mbd_ok, 1)

                def exponent(t, q, i):
                    dve.wait_ge(spread, t + 1)
                    dve.tensor_tensor(arg[q][:, :, :], ps_e[:, 0:J * H].rearrange("p (j h) -> p j h", h=H),
                                      rows[q][:, :, D:C0], ALU.subtract).then_inc(diff_ok, 1)

                def weigh(t, q, i):
                    dve.wait_ge(exp_ok, t + 1)
                    dve.tensor_tensor(msg[q][:, :, 0:D].rearrange("p j (h d) -> p j h d", h=H),
                                      rows[q][:, :, 0:D].rearrange("p j (h d) -> p j h d", h=H),
                                      msg[q][:, :, D:C0].unsqueeze(3).broadcast_to([P, J, H, HD]), ALU.mult).then_inc(msg_ok, 1)

                def add(t, q, i):
                    window = G.acc[0:C0, bass.ds(windows.base(), W)]
                    dve.wait_ge(added, t) if later(t, 1) else None
                    dve.wait_ge(summed, t + 1)
                    dve.tensor_tensor(window, window, ps_w[0:C0, 0:W], ALU.add).then_inc(added, 1)
                windows = WindowBases(nc, mybir.EngineType.DVE, S, G, R)
                pipeline(dve, S.T, [(2, add_counts), (7, exponent), (6, mask_maxima), (2, attend), (4, merge), (5, take_maxima),
                                    (3, reduce), (7, weigh), (0, build), (8, add)], R, windows)
                next_window(dve, G, moved_on)

            @block.scalar
            def _(act):
                def take_index(t, q, i):
                    if later(t, R):
                        act.wait_ge(rows_in[q], 16 * J * i)
                        act.sem_inc(indexing, 1)
                    act.copy(index[q][:, :], G.src_i[:, bass.ds(t * J, J)]).then_inc(index_ok, 1)

                def source_rows(t, q, i):
                    if later(t, 2):
                        act.wait_ge(src_ok, t - 1)
                        act.sem_inc(apart, 1)
                    for j in range(J):
                        ins = act.activation(away[q][:, j, :], G.iota_p[:, :], ACT.Abs, bias=G.src_neg[:, bass.ds(t, 1), j])
                    ins.then_inc(away_ok, 1)
                    if later(t, 2):
                        act.wait_ge(adj_mm, t - 1)
                    act.wait_ge(away_ok, t + 1)
                    act.activation(ohsrc[q][:, :, :], away[q][:, :, :], ACT.Relu, bias=1.0, scale=-1.0).then_inc(src_ok, 1)

                def evacuate(t, q, i):
                    if later(t, R):
                        act.wait_ge(spread, t - R + 1)
                    act.wait_ge(turned, 2 * (t + 1))
                    act.copy(ohT[q][:, :], ps_t[0:JW, 0:P]).then_inc(evac, 1)
                    if later(t, 2):
                        act.wait_ge(scored, t - 1)
                    act.copy(eaT[q][:, :], ps_t[0:J * 16, P:2 * P]).then_inc(evac, 1)

                def exponential(t, q, i):
                    if later(t, 2):
                        act.wait_ge(summed, t - 1)
                    act.wait_ge(diff_ok, t + 1)
                    act.activation(arg[q][:, :, :], arg[q][:, :, :], ACT.Relu).then_inc(arg_ok, 1)
                    act.wait_ge(arg_ok, t + 1)
                    act.activation(msg[q][:, :, D:C0], arg[q][:, :, :], ACT.Exp, scale=-1.0).then_inc(exp_ok, 1)
                pipeline(act, S.T, [(0, take_index), (3, evacuate), (9, exponential), (2, source_rows)], R)

            @block.tensor
            def _(pe):
                def spread_window(t, q, i):
                    if later(t, 1):
                        pe.wait_ge(mbd_ok, t)
                    pe.wait_ge(mrep_ok, t + 1)
                    pe.matmul(ps_x[0:JW, W:W + H], mrep[q][:, :, :].rearrange("h j w -> h (j w)"), G.ident[0:H, 0:H],
                              start=True, stop=True).then_inc(mspread, 1)

                def turn(t, q, i):
                    pe.wait_ge(ea_in[q], edges_landed(S, t, i))
                    if later(t, 1):
                        pe.wait_ge(evac, 2 * t)
                    pe.wait_ge(oh_ok, t + 1)
                    pe.transpose(ps_t[0:JW, 0:P], oh[q][:, :, :].rearrange("p j w -> p (j w)"), G.ident[:, :]).then_inc(turned, 1)
                    last = isinstance(t, int) and t == S.TF
                    pe.transpose(ps_t[0:J * 16, P:2 * P], (ea_last if last else ea[q])[:, :], G.ident[:, :]).then_inc(turned, 1)

                def count(t, q, i):
                    pe.wait_ge(src_ok, t + 1)
                    if later(t, 1):
                        pe.wait_ge(adj_ok, t)
                    pe.wait_ge(key_ok, t + 1)
                    for j in range(J):
                        for k in (0, 1):
                            ins = pe.matmul(ps_a[:, 512 * k:512 * k + HALF], ohsrc[q][:, j, :], ohkey[q][j][:, k * HALF:(k + 1) * HALF],
                                            start=(j == 0), stop=(j == J - 1))
                    ins.then_inc(adj_mm, 1)

                def score_edges(t, q, i):
                    pe.wait_ge(evac, 2 * (t + 1))
                    if later(t, 1):
                        pe.wait_ge(score_ok, t)
                    pe.wait_ge(winbd_ok, t + 1)
                    out = ps_s[:, 0:J * H]
                    pe.matmul(out, ohT[q][:, :], winbd[q][:, :, :].rearrange("p j h -> p (j h)"), start=True, stop=False)
                    pe.matmul(out, eaT[q][:, :], G.w_edge16[0:J * 16, :], start=False, stop=True).then_inc(scored, 1)

                def turn_masked(t, q, i):
                    if later(t, 1):
                        pe.wait_ge(mcol_ok, t)
                    pe.wait_ge(masked_ok, t + 1)
                    for j in range(J):
                        ins = pe.transpose(ps_m[0:H * W, j * P:(j + 1) * P], masked[q][:, j, :, :].rearrange("p h w -> p (h w)"), G.ident[:, :])
                    ins.then_inc(mask_turned, 1)

                def window_maxima(t, q, i):
                    if later(t, 1):
                        pe.wait_ge(merged, t)
                    if later(t, 3):
                        pe.wait_ge(mbd_ok, t - 2)
                    pe.wait_ge(mdiag_ok, t + 1)
                    pe.matmul(ps_x[0:H, 0:W], G.blockmask[0:H * W, :, 0], mdiag[q][:, :], start=True, stop=True).then_inc(maxima, 1)

                def spread_maxima(t, q, i):
                    if later(t, 1):
                        pe.wait_ge(diff_ok, t)
                    pe.wait_ge(mbd_ok, t + 1)
                    pe.matmul(ps_e[:, 0:J * H], ohT[q][:, :], mbd[q][:, :, :].rearrange("p j h -> p (j h)"),
                              start=True, stop=True).then_inc(spread, 1)

                def scatter(t, q, i):
                    if later(t, 1):
                        pe.wait_ge(added, t)
                    pe.wait_ge(msg_ok, t + 1)
                    for j in range(J):
                        ins = pe.matmul(ps_w[0:C0, 0:W], msg[q][:, j, :], oh[q][:, j, :], start=(j == 0), stop=(j == J - 1))
                    ins.then_inc(summed, 1)
                pipeline(pe, S.T, [(1, turn), (8, scatter), (1, count), (6, spread_maxima), (1, score_edges), (3, window_maxima),
                                   (5, spread_window), (2, turn_masked)], R)


def attention_nodes_phase(nc, S, G, table0):
    C0 = D + H
    PER = 512 // C0
    NG = -(-S.NB // PER)
    with ExitStack() as ctx:
        sb = lambda name, shape, dt: ctx.enter_context(nc.sbuf_tensor(name, shape, dt))
        sem = phase_semaphores(nc, ctx)
        h = sb("n_h", [P, S.NB, D], F32)
        sums = sb("n_sums", [P, S.NB, C0], F32)
        ps = [ctx.enter_context(nc.psum_tensor(f"ps_n{g}", [P, 512], F32)) for g in range(NG)]
        h_in, turned, chain = sem("n_h_in"), sem("n_turned"), sem("n_chain")
        with nc.Block() as block:
            @block.sync
            def _(sp):
                sp.dma_start(h[:, :, :], node_view(table0, S)[:, :, 0:D]).then_inc(h_in, 16)
                sp.wait_ge(h_in, 16)

            @block.tensor
            def _(pe):
                for b in range(S.NB):
                    g, k = divmod(b, PER)
                    pe.transpose(ps[g][:, k * C0:(k + 1) * C0], G.acc[0:C0, b * P:(b + 1) * P], G.ident[0:C0, 0:C0]).then_inc(turned, 1)

            @block.vector
            def _(dve):
                link = Chain(dve, chain)
                for g in range(NG):
                    b0, b1 = g * PER, min((g + 1) * PER, S.NB)
                    dve.wait_ge(turned, b1)
                    link(dve.tensor_copy(sums[:, b0:b1, :], ps[g][:, 0:(b1 - b0) * C0].rearrange("p (b c) -> p b c", c=C0)))
                link(dve.tensor_scalar(sums[:, :, D:C0], sums[:, :, D:C0], 1e-8, None, ALU.add))
                link(dve.reciprocal(sums[:, :, D:C0], sums[:, :, D:C0]))
                for k in range(H):
                    link(dve.tensor_tensor(G.y[:, :, k * HD:(k + 1) * HD], sums[:, :, k * HD:(k + 1) * HD],
                                           sums[:, :, D + k:D + k + 1].broadcast_to([P, S.NB, HD]), ALU.mult))
                dve.wait_ge(h_in, 16)
                link(dve.tensor_tensor(G.y[:, :, :], G.y[:, :, :], h[:, :, :], ALU.add))


def norm_phase(nc, S, G, tag, affine, out):
    with ExitStack() as ctx:
        sb = lambda name, shape, dt: ctx.enter_context(nc.sbuf_tensor(name + tag, shape, dt))
        sem = phase_semaphores(nc, ctx, tag)
        centred, square = sb("centred", [P, S.NB, D], F32), sb("square", [P, S.NB, D], F32)
        mean, var, std, inv = (sb(n, [P, S.NB], F32) for n in ("mean", "var", "std", "inv"))
        chain, var_ok, std_ok = sem("nchain"), sem("var_ok"), sem("std_ok")
        wide = lambda a: a[:, :].unsqueeze(2).broadcast_to([P, S.NB, D])
        with nc.Block() as block:
            @block.vector
            def _(dve):
                link = Chain(dve, chain)
                link(dve.reduce_sum(mean[:, :], G.y[:, :, :], axis=AX.X))
                link(dve.tensor_scalar(mean[:, :], mean[:, :], 1.0 / D, None, ALU.mult))
                link(dve.tensor_tensor(centred[:, :, :], G.y[:, :, :], wide(mean), ALU.subtract))
                link(dve.tensor_tensor(square[:, :, :], centred[:, :, :], centred[:, :, :], ALU.mult))
                link(dve.reduce_sum(var[:, :], square[:, :, :], axis=AX.X))
                link(dve.tensor_scalar(var[:, :], var[:, :], 1.0 / D, 1e-5, ALU.mult, ALU.add))
                dve.sem_inc(var_ok, 1)
                dve.wait_ge(std_ok, 1)
                link(dve.reciprocal(inv[:, :], std[:, :]))
                if affine:
                    link(dve.tensor_tensor(centred[:, :, :], centred[:, :, :], wide(inv), ALU.mult))
                    row = lambda a: a.unsqueeze(1).broadcast_to([P, S.NB, D])
                    link(dve.tensor_tensor(centred[:, :, :], centred[:, :, :], row(G.gamma), ALU.mult))
                    link(dve.tensor_tensor(centred[:, :, :], centred[:, :, :], row(G.beta), ALU.add))
                    link(dve.tensor_tensor(out[:, :, :], centred[:, :, :], G.x[:, :, :], ALU.add))
                else:
                    link(dve.tensor_tensor(out[:, :, :], centred[:, :, :], wide(inv), ALU.mult))

            @block.scalar
            def _(act):
                act.wait_ge(var_ok, 1)
                act.activation(std[:, :], var[:, :], ACT.Sqrt).then_inc(std_ok, 1)


def widen_block(eng, copy, S, adj, wide, m, b0, b1):
    return copy(wide[:, b0:b1, :], adj[:, b0:b1, bass.ds(m * P, P)])


def count_product_phase(nc, S, G, tag, adj, parts, agg, wide_adj):
    A = (S.NB + 1) // 2
    with ExitStack() as ctx:
        sem = phase_semaphores(nc, ctx, tag)
        ps = [ctx.enter_context(nc.psum_tensor(f"ps_p{tag}{u}", [P, 512], F32)) for u in (0, 1)]
        product, taken, by_act, by_dve = (sem(n) for n in ("product", "taken", "by_act", "by_dve"))
        with nc.Block() as block:
            @block.tensor
            def _(pe):
                def multiply(m, u, i):
                    if later(m, 2):
                        pe.wait_ge(taken, m - 1)
                    pe.wait_ge(by_dve, m + 1)
                    pe.wait_ge(by_act, m + 1)
                    for b in range(S.NB):
                        ins = pe.matmul(ps[u][:, 0:1] if parts is None else ps[u][:, 0:3 * D], wide_adj[u][:, b, :],
                                        G.ones_bf[:, 0:1] if parts is None else parts[:, b, :], start=(b == 0), stop=(b == S.NB - 1))
                    ins.then_inc(product, 1)
                blocks(pe, S.NB, multiply)

            @block.scalar
            def _(act):
                def widen(m, u, i):
                    if later(m, 2):
                        act.wait_ge(product, m - 1)
                    widen_block(act, act.copy, S, adj, wide_adj[u], m, 0, A).then_inc(by_act, 1)
                blocks(act, S.NB, widen)

            @block.vector
            def _(dve):
                def take(m, u):
                    dve.wait_ge(product, m + 1)
                    if parts is None:
                        dve.tensor_copy(agg[:, bass.ds(m, 1), 0], ps[u][:, 0:1]).then_inc(taken, 1)
                    else:
                        dve.reduce_sum(agg[:, bass.ds(m, 1), :].rearrange("p o c -> p (o c)"),
                                       ps[u][:, 0:3 * D].rearrange("p (s c) -> p c s", c=D), axis=AX.X).then_inc(taken, 1)

                def step(m, u, i):
                    if later(m, 2):
                        dve.wait_ge(product, m - 1)
                    widen_block(dve, dve.tensor_copy, S, adj, wide_adj[u], m, A, S.NB).then_inc(by_dve, 1)
                    if later(m, 1):
                        take(m - 1, 1 - u)
                blocks(dve, S.NB, step)
                take(S.NB - 1, (S.NB - 1) % 2)
                dve.wait_ge(taken, S.NB)


def count_check_phase(nc, S, G, agg):
    with ExitStack() as ctx:
        sem = phase_semaphores(nc, ctx)
        total, ones = (ctx.enter_context(nc.sbuf_tensor(n, [P, 1], F32)) for n in ("c_total", "c_ones"))
        ps = ctx.enter_context(nc.psum_tensor("ps_check", [P, 512], F32))
        chain, summed = sem("c_chain"), sem("c_summed")
        with nc.Block() as block:
            @block.vector
            def _(dve):
                link = Chain(dve, chain)
                link(dve.memset(ones[:, :], 1.0))
                link(dve.reduce_sum(total[:, :], agg[:, :, 0], axis=AX.X))
                dve.wait_ge(summed, 1)
                link(dve.tensor_scalar(G.control[:, 2:3], ps[0:1, 0:1], float(S.E), None, ALU.not_equal))

            @block.tensor
            def _(pe):
                pe.wait_ge(chain, 2)
                pe.matmul(ps[0:1, 0:1], total[:, :], ones[:, :], start=True, stop=True).then_inc(summed, 1)


def sparse_sum(nc, S, G, tag, agg, src_features, gather_index, scatter_index, table, room):
    rel, window = room("z_rel" + tag, [P, S.T * J], F32), room("z_window" + tag, [P, W], F32)
    feats = room("z_feats" + tag, [P, S.NB, D], F32)
    index = [room(f"z_index{q}" + tag, [P, J], I32) for q in range(4)]
    rows = [room(f"z_rows{q}" + tag, [P, J, D], F32) for q in range(4)]
    oh = [room(f"z_oh{q}" + tag, [P, J, W], F32) for q in range(4)]
    with ExitStack() as ctx:
        sem = phase_semaphores(nc, ctx, tag)
        chain, stored = sem("z_chain"), sem("z_stored")
        with nc.Block() as block:
            @block.vector
            def _(dve):
                link = Chain(dve, chain)
                if src_features is None:
                    link(dve.memset(feats[:, :, :], 1.0))
                else:
                    link(dve.tensor_copy(feats[:, :, :], src_features[:, :, :]))
                link(dve.tensor_copy(rel[:, :], scatter_index[:, :]))
                link(dve.tensor_tensor(rel[:, :], rel[:, :], G.real[:, :], ALU.mult))
                link(dve.tensor_tensor(rel[:, :], rel[:, :], G.real[:, :], ALU.add))
                link(dve.tensor_scalar(rel[:, :], rel[:, :], -1.0, None, ALU.add))
                link(dve.tensor_copy(window[:, :], G.iota_w[:, :]))

            @block.sync
            def _(sp):
                sp.wait_ge(chain, 6)
                sp.dma_start(node_view(table, S), feats[:, :, :]).then_inc(stored, 16)
                sp.wait_ge(stored, 16)
    with nc.Fori(0, S.NW) as p, ExitStack() as ctx:
        sem = phase_semaphores(nc, ctx, tag)
        ring = lambda f: [f(q) for q in range(4)]
        ps = ctx.enter_context(nc.psum_tensor("ps_z" + tag, [P, 512], F32))
        rows_in = ring(lambda q: sem(f"z_ri{q}"))
        index_ok, oh_ok, summed, moved, gathering, indexing = (sem("z_" + n) for n in ("idx", "oh", "sum", "mvd", "gat", "ing"))
        with nc.Block() as block:
            @block.scalar
            def _(act):
                def take_index(t, q, i):
                    if later(t, 4):
                        act.wait_ge(rows_in[q], 16 * J * i)
                        act.sem_inc(indexing, 1)
                    act.copy(index[q][:, :], gather_index[:, bass.ds(t * J, J)]).then_inc(index_ok, 1)
                pipeline(act, S.T, [(0, take_index)])

            @block.gpsimd
            def _(pool):
                def gather(t, q, i):
                    pool.wait_ge(index_ok, t + 1)
                    if later(t, 4):
                        pool.wait_ge(summed, t - 3)
                    pool.sem_inc(gathering, 1)
                    for j in range(J):
                        pool.indirect_dma_start(rows[q][:, j, :], None, table, bass.IndirectOffsetOnAxis(
                            ap=index[q][:, j:j + 1], axis=0)).then_inc(rows_in[q], 16)
                pipeline(pool, S.T, [(0, gather)])

            @block.vector
            def _(dve):
                def build(t, q, i):
                    if later(t, 4):
                        dve.wait_ge(summed, t - 3)
                    dve.tensor_tensor(oh[q][:, :, :], rel[:, bass.ds(t * J, J)].unsqueeze(2).broadcast_to([P, J, W]),
                                      window[:, :].unsqueeze(1).broadcast_to([P, J, W]), ALU.is_equal).then_inc(oh_ok, 1)
                pipeline(dve, S.T, [(0, build)])
                dve.wait_ge(summed, S.T)
                dve.tensor_copy(G.acc[0:D, bass.ds(p * W, W)], ps[0:D, 0:W]).then_inc(moved, 1)
                dve.tensor_scalar(window[:, :], window[:, :], float(W), None, ALU.add).then_inc(moved, 1)
                dve.wait_ge(moved, 2)

            @block.tensor
            def _(pe):
                def scatter(t, q, i):
                    pe.wait_ge(oh_ok, t + 1)
                    pe.wait_ge(rows_in[q], 16 * J * (i + 1))
                    for j in range(J):
                        first, last = isinstance(t, int) and t == 0 and j == 0, isinstance(t, int) and t == S.T - 1 and j == J - 1
                        ins = pe.matmul(ps[0:D, 0:W], rows[q][:, j, :], oh[q][:, j, :], start=first, stop=last)
                    ins.then_inc(summed, 1)
                pipeline(pe, S.T, [(0, scatter)])
    with ExitStack() as ctx:
        sem = phase_semaphores(nc, ctx, tag)
        ps = [ctx.enter_context(nc.psum_tensor(f"ps_zt{tag}{u}", [P, 512], F32)) for u in (0, 1)]
        turned, taken = sem("z_turned"), sem("z_taken")
        with nc.Block() as block:
            @block.tensor
            def _(pe):
                for b in range(S.NB):
                    if b >= 2:
                        pe.wait_ge(taken, b - 1)
                    pe.transpose(ps[b % 2][:, 0:D], G.acc[0:D, b * P:(b + 1) * P], G.ident[0:D, 0:D]).then_inc(turned, 1)

            @block.vector
            def _(dve):
                for b in range(S.NB):
                    dve.wait_ge(turned, b + 1)
                    dve.tensor_copy(agg[:, b, :], ps[b % 2][:, 0:D]).then_inc(taken, 1)
                dve.wait_ge(taken, S.NB)


def propagate_nodes_phase(nc, S, G, tag, k, theta, agg, feat, source, parts, deg, dinv):
    wide = lambda a: a[:, :].unsqueeze(2).broadcast_to([P, S.NB, D])
    with ExitStack() as ctx:
        sem = phase_semaphores(nc, ctx, tag)
        chain, deg_ok, sqrt_ok = sem("pchain"), sem("deg_ok"), sem("sqrt_ok")
        with nc.Block() as block:
            @block.scalar
            def _(act):
                if k == 0:
                    act.wait_ge(deg_ok, 1)
                    act.activation(dinv[:, :], deg[:, :], ACT.Sqrt).then_inc(sqrt_ok, 1)

            @block.vector
            def _(dve):
                link = Chain(dve, chain)
                if k == 0:
                    link(dve.tensor_scalar(deg[:, :], agg[:, :, 0], 1.0, None, ALU.max))
                    dve.sem_inc(deg_ok, 1)
                    dve.wait_ge(sqrt_ok, 1)
                    link(dve.reciprocal(dinv[:, :], dinv[:, :]))
                    link(dve.tensor_copy(feat[:, :, :], G.x[:, :, :]))
                    if theta:
                        link(dve.reciprocal(G.inv_cnt[:, :], deg[:, :]))
                        link(dve.tensor_scalar(G.y[:, :, :], G.x[:, :, :], 1.0 + theta[0], None, ALU.mult))
                    else:
                        link(dve.tensor_scalar(deg[:, :], agg[:, :, 0], 0.0, None, ALU.is_gt))
                        link(dve.tensor_tensor(dinv[:, :], dinv[:, :], deg[:, :], ALU.mult))
                        link(dve.tensor_copy(G.y[:, :, :], G.x[:, :, :]))
                else:
                    link(dve.tensor_tensor(agg[:, :, :], agg[:, :, :], wide(dinv), ALU.mult))
                    if theta:
                        link(dve.tensor_tensor(feat[:, :, :], feat[:, :, :], agg[:, :, :], ALU.subtract))
                        link(dve.scalar_tensor_tensor(G.y[:, :, :], feat[:, :, :], theta[k], G.y[:, :, :], ALU.mult, ALU.add))
                    else:
                        link(dve.tensor_tensor(feat[:, :, :], agg[:, :, :], wide(dinv), ALU.mult))
                        link(dve.tensor_tensor(G.y[:, :, :], G.y[:, :, :], feat[:, :, :], ALU.add))
                if k < 3:
                    if theta:
                        link(dve.tensor_tensor(source[:, :, :], feat[:, :, :], wide(dinv), ALU.mult))
                    link(dve.tensor_copy(parts[:, :, 0:D], source[:, :, :]))
                    link(dve.tensor_tensor(agg[:, :, :], source[:, :, :], parts[:, :, 0:D], ALU.subtract))
                    link(dve.tensor_copy(parts[:, :, D:2 * D], agg[:, :, :]))
                    link(dve.tensor_tensor(agg[:, :, :], agg[:, :, :], parts[:, :, D:2 * D], ALU.subtract))
                    link(dve.tensor_copy(parts[:, :, 2 * D:3 * D], agg[:, :, :]))
                elif not theta:
                    link(dve.scalar_tensor_tensor(G.y[:, :, :], G.y[:, :, :], 0.25, G.x[:, :, :], ALU.mult, ALU.add))


def propagate(nc, S, G, tag, adj, theta, gather_index, scatter_index, table, room):
    parts = room("parts" + tag, [P, S.NB, 3 * D], BF16)
    agg, feat = (room(n + tag, [P, S.NB, D], F32) for n in ("agg", "feat"))
    source = room("source" + tag, [P, S.NB, D], F32) if theta else feat
    deg, dinv = room("deg" + tag, [P, S.NB], F32), room("dinv" + tag, [P, S.NB], F32)
    wide_adj = [room(f"wide{u}" + tag, [P, S.NB, P], BF16) for u in (0, 1)]
    for k in range(4):
        count_product_phase(nc, S, G, f"{tag}_{k}", adj, parts if k else None, agg, wide_adj)
        if k == 0 and theta:
            count_check_phase(nc, S, G, agg)
        overflow = nc.values_load(G.control[0:1, 2:3], min_val=0, max_val=1)
        with nc.If(overflow > 0), ExitStack() as own:
            nc.all_engine_barrier()
            sparse_sum(nc, S, G, f"{tag}_{k}s", agg, source if k else None, gather_index, scatter_index, table,
                       (lambda n, s, d: own.enter_context(nc.sbuf_tensor(n, s, d))) if theta else room.again)
        nc.end_ifs()
        nc.all_engine_barrier()
        propagate_nodes_phase(nc, S, G, f"{tag}_{k}", k, theta, agg, feat, source, parts, deg, dinv)


def transpose_counts_phase(nc, S, G, adj, adjT):
    PER = 4
    NG = -(-S.NB // PER)
    A = S.NB * 2 // 5
    with ExitStack() as ctx:
        sem = phase_semaphores(nc, ctx)
        ps = [ctx.enter_context(nc.psum_tensor(f"ps_tc{g}", [P, 512], F32)) for g in range(NG)]
        wide_adj = [ctx.enter_context(nc.sbuf_tensor("tc_wide", [P, S.NB, P], BF16)),
                    G.y[:, :, :].rearrange("p b c -> p (b c)").bitcast(BF16).rearrange("p (b c) -> p b c", c=P)]
        wide_act, wide_dve, turned, by_act, by_dve = (sem("tc_" + n) for n in ("wide_act", "wide_dve", "turned", "by_act", "by_dve"))
        n_act, n_dve = len(range(0, NG, 2)), len(range(1, NG, 2))

        def widen(eng, copy, widened, m, u, b0, b1):
            if later(m, 2):
                eng.wait_ge(turned, (m - 1) * NG)
            widen_block(eng, copy, S, adj, wide_adj[u], m, b0, b1).then_inc(widened, 1)

        def evacuate(eng, copy, done, widened, first, b0, b1):
            def take(m):
                for g in range(first, NG, 2):
                    c0, c1 = g * PER, min((g + 1) * PER, S.NB)
                    eng.wait_ge(turned, m * NG + g + 1)
                    copy(adjT[:, bass.ds(m, 1), c0 * P:c1 * P].rearrange("p o c -> p (o c)"), ps[g][:, 0:(c1 - c0) * P]).then_inc(done, 1)

            def step(m, u, i):
                widen(eng, copy, widened, m, u, b0, b1)
                if later(m, 1):
                    take(m - 1)
            blocks(eng, S.NB, step)
            take(S.NB - 1)

        with nc.Block() as block:
            @block.tensor
            def _(pe):
                def step(m, u, i):
                    pe.wait_ge(wide_act, m + 1)
                    pe.wait_ge(wide_dve, m + 1)
                    for g in range(NG):
                        if later(m, 1):
                            if g % 2:
                                pe.wait_ge(by_dve, (m - 1) * n_dve + g // 2 + 1)
                            else:
                                pe.wait_ge(by_act, (m - 1) * n_act + g // 2 + 1)
                        for b in range(g * PER, min((g + 1) * PER, S.NB)):
                            ins = pe.matmul(ps[g][:, (b % PER) * P:(b % PER + 1) * P], wide_adj[u][:, b, :], G.ident_bf[:, :],
                                            start=True, stop=True)
                        ins.then_inc(turned, 1)
                blocks(pe, S.NB, step)

            @block.scalar
            def _(act):
                evacuate(act, act.copy, by_act, wide_act, 0, 0, A)

            @block.vector
            def _(dve):
                evacuate(dve, dve.tensor_copy, by_dve, wide_dve, 1, A, S.NB)


def edge_phase(nc, S, G, tag, table, target_table, w_edge, w_msg, edges, known=None, keep=None):
    L = len(w_edge)
    cols = (L + 1) * D
    with ExitStack() as ctx:
        sb = lambda name, shape, dt: ctx.enter_context(nc.sbuf_tensor(name + tag, shape, dt))
        pb = lambda name: ctx.enter_context(nc.psum_tensor(name + tag, [P, 512], F32))
        sem = phase_semaphores(nc, ctx, tag)
        R = 6
        ring = lambda f: [f(q) for q in range(R)]
        three = lambda f: [f(q) for q in range(3)] * (R // 3)
        per_level = lambda f, n=L: [f(k) for k in range(n)]
        C = J * D
        half = lambda a, k: a[:, k * P:(k + 1) * P]
        if known is None:
            ea, ea_last = ring(lambda q: sb(f"e_ea{q}", [P, C], F32)), sb("e_ea_last", [P, C], F32)
        rows = ring(lambda q: sb(f"e_rows{q}", [P, J, cols], F32))
        index = ring(lambda q: sb(f"e_index{q}", [P, J], I32))
        oh = ring(lambda q: sb(f"e_oh{q}", [P, J, W], F32))
        ohT = ring(lambda q: sb(f"e_ohT{q}", [JW, P], F32)) if L else None
        win = ring(lambda q: sb(f"e_win{q}", [JW, L * D], F32)) if L else None
        winbd = per_level(lambda k: ring(lambda q: sb(f"e_winbd{k}_{q}", [JW, J, D], F32)))
        new = per_level(lambda k: three(lambda q: sb(f"e_new{k}_{q}", [P, J, D], F32)))
        featT = per_level(lambda k: ring(lambda q: sb(f"e_featT{k}_{q}", [P, C], F32)), L + 1)
        msg = three(lambda q: sb(f"e_msg{q}", [P, J, D], F32))
        ps_t = pb("ps_t")
        ps_u, ps_n = per_level(lambda k: pb(f"ps_u{k}")), per_level(lambda k: pb(f"ps_n{k}"))
        ps_m, ps_w = pb("ps_m"), pb("ps_w")
        ea_in, win_in, rows_in = (ring(lambda q: sem(f"e_{n}{q}_")) for n in ("ea", "wi", "ri"))
        index_ok, indexing, gathering, oh_ok, winbd_ok, turned, cleared, moved_on = (
            sem("e_" + n + "_") for n in ("idx", "ing", "gat", "oh", "wbd", "turned", "clr", "moved_on"))
        updated, new_pre, new_ok, new_turned = (per_level(lambda k: sem(f"e_{n}{k}_")) for n in ("upd", "npre", "new", "nturn"))
        featT_ok = per_level(lambda k: sem(f"e_featT{k}_"), L + 1)
        ohT_ok, msg_mm, msg_pre, msg_ok, summed, added = (sem("e_" + n + "_") for n in ("ohT", "mm", "mpre", "msg", "sum", "add"))

        kept = ring(lambda q: sem(f"e_kept{q}_")) if keep is not None else None
        turn_at, update_at, sources_at, turn_new_at = 2, per_level(lambda k: 3 + 3 * k), per_level(lambda k: 4 + 3 * k), per_level(lambda k: 5 + 3 * k)
        messages_at, message_at, scatter_at, add_at = 3 + 3 * L, 4 + 3 * L, 5 + 3 * L, 6 + 3 * L

        def halves(stages, lead=0):
            return [(h // 2 + lead, step) for h, step in [s for s in stages if s[0] % 2 == 0] + [s for s in stages if s[0] % 2]]

        with nc.Block() as block:
            @block.sync
            def _(sp):
                def load(t, q, i):
                    if later(t, R):
                        sp.wait_ge(turned if known is None else updated[0], t - R + 1)
                        if L:
                            sp.wait_ge(winbd_ok, t - R + 1)
                    elif known is None and isinstance(t, int) and t == 0:
                        sp.wait_ge(cleared, 1)
                    if known is None:
                        load_edges(sp, S, ea[q], ea_last, edges, t, ea_in[q])
                    else:
                        sp.dma_start(featT[0][q][:, :], known[bass.ds(t * P, P), :]).then_inc(ea_in[q], 16)
                    if L:
                        sp.dma_start(win[q][:, :], window_copy(target_table, window_base(sp, S, G, t))).then_inc(win_in[q], 16)

                def keep_features(t, q, i):
                    sp.wait_ge(featT_ok[L], t + 1)
                    sp.dma_start(keep[bass.ds(t * P, P), :], featT[L][q][:, :]).then_inc(kept[q], 16)
                pipeline(sp, S.T, [(0, load)] + ([(R - 1, keep_features)] if keep is not None else []), R)
                if keep is not None:
                    for q in range(R):
                        sp.wait_ge(kept[q], 16 * len(range(q, S.T, R)))

            @block.gpsimd
            def _(pool):
                if known is None:
                    pool.memset(ea_last[:, :], 0.0).then_inc(cleared, 1)

                def gather(t, q, i):
                    pool.wait_ge(index_ok, t + 1)
                    if later(t, R):
                        pool.wait_ge(msg_pre, t - R + 1)
                    pool.sem_inc(gathering, 1)
                    for j in range(J):
                        pool.indirect_dma_start(rows[q][:, j, :], None, table, bass.IndirectOffsetOnAxis(
                            ap=index[q][:, j:j + 1], axis=0)).then_inc(rows_in[q], 16)
                pipeline(pool, S.T, [(0, gather)], R)

            @block.vector
            def _(dve):
                def build(t, q, i):
                    if later(t, R):
                        dve.wait_ge(summed, t - R + 1)
                    one_hot(dve, S, G, oh[q][:, :, :], t).then_inc(oh_ok, 1)
                    if L:
                        dve.wait_ge(win_in[q], 16 * (i + 1))
                        if later(t, R):
                            dve.wait_ge(updated[L - 1], t - R + 1)
                        for k in range(L):
                            ins = dve.tensor_tensor(winbd[k][q][:, :, :], win[q][:, k * D:(k + 1) * D].unsqueeze(1).broadcast_to([JW, J, D]),
                                                    G.blockmask[0:JW, :, :].broadcast_to([JW, J, D]), ALU.mult)
                        ins.then_inc(winbd_ok, 1)

                def add_sources(k):
                    def step(t, q, i):
                        dve.wait_ge(rows_in[q], 16 * J * (i + 1))
                        if later(t, 3):
                            dve.wait_ge(new_turned[k], t - 2)
                        dve.wait_ge(updated[k], t + 1)
                        dve.tensor_tensor(new[k][q][:, :, :], ps_u[k][:, 0:C].rearrange("p (j c) -> p j c", j=J),
                                          rows[q][:, :, k * D:(k + 1) * D], ALU.add).then_inc(new_pre[k], 1)
                    return step

                def add_message(t, q, i):
                    dve.wait_ge(rows_in[q], 16 * J * (i + 1))
                    if later(t, 3):
                        dve.wait_ge(summed, t - 2)
                    dve.wait_ge(msg_mm, t + 1)
                    dve.tensor_tensor(msg[q][:, :, :], ps_m[:, 0:C].rearrange("p (j c) -> p j c", j=J),
                                      rows[q][:, :, cols - D:cols], ALU.add).then_inc(msg_pre, 1)

                def add(t, q, i):
                    window = G.acc[0:D, bass.ds(windows.base(), W)]
                    if later(t, 1):
                        dve.wait_ge(added, t)
                    dve.wait_ge(summed, t + 1)
                    dve.tensor_tensor(window, window, ps_w[0:D, 0:W], ALU.add).then_inc(added, 1)
                windows = WindowBases(nc, mybir.EngineType.DVE, S, G, R)
                pipeline(dve, S.T, halves([(sources_at[k], add_sources(k)) for k in range(L)] +
                                          [(message_at, add_message), (1, build), (add_at, add)]), R, windows)
                dve.wait_ge(added, S.T)
                next_window(dve, G, moved_on)

            @block.scalar
            def _(act):
                def take_index(t, q, i):
                    if later(t, R):
                        act.wait_ge(rows_in[q], 16 * J * i)
                        act.sem_inc(indexing, 1)
                    act.copy(index[q][:, :], G.src_i[:, bass.ds(t * J, J)]).then_inc(index_ok, 1)

                def evacuate(t, q, i):
                    act.wait_ge(turned, t + 1)
                    if later(t, R):
                        act.wait_ge(updated[L - 1] if L else msg_mm, t - R + 1)
                    if L:
                        act.copy(ohT[q][:, :], ps_t[0:JW, C:C + P]).then_inc(ohT_ok, 1)
                    if known is None:
                        act.copy(featT[0][q][:, :], ps_t[:, 0:C]).then_inc(featT_ok[0], 1)

                def relu_new(k):
                    def step(t, q, i):
                        act.wait_ge(new_pre[k], t + 1)
                        act.activation(new[k][q][:, :, :], new[k][q][:, :, :], ACT.Relu).then_inc(new_ok[k], 1)
                    return step

                def evacuate_new(k):
                    def step(t, q, i):
                        if later(t, R):
                            act.wait_ge(updated[k + 1] if k + 1 < L else msg_mm, t - R + 1)
                            if keep is not None and k == L - 1:
                                act.wait_ge(kept[q], 16 * i)
                        act.wait_ge(new_turned[k], t + 1)
                        act.copy(featT[k + 1][q][:, :], ps_n[k][:, 0:C]).then_inc(featT_ok[k + 1], 1)
                    return step

                def relu_message(t, q, i):
                    act.wait_ge(msg_pre, t + 1)
                    act.activation(msg[q][:, :, :], msg[q][:, :, :], ACT.Relu).then_inc(msg_ok, 1)
                lead = 2
                stages = [(turn_at, evacuate)]
                for k in range(L):
                    stages += [(sources_at[k], relu_new(k)), (turn_new_at[k], evacuate_new(k))]
                pipeline(act, S.T, [(0, take_index)] + halves(stages + [(message_at, relu_message)], lead), R)

            @block.tensor
            def _(pe):
                def turn(t, q, i):
                    if known is not None:
                        if later(t, 1):
                            pe.wait_ge(ohT_ok, t)
                        pe.wait_ge(oh_ok, t + 1)
                        pe.transpose(ps_t[0:JW, C:C + P], oh[q][:, :, :].rearrange("p j w -> p (j w)"), G.ident[:, :]).then_inc(turned, 1)
                        return
                    pe.wait_ge(ea_in[q], edges_landed(S, t, i))
                    if later(t, 1):
                        pe.wait_ge(featT_ok[0], t)
                    if L:
                        pe.wait_ge(oh_ok, t + 1)
                        pe.transpose(ps_t[0:JW, C:C + P], oh[q][:, :, :].rearrange("p j w -> p (j w)"), G.ident[:, :])
                    a = ea_last if isinstance(t, int) and t == S.TF else ea[q]
                    pe.transpose(ps_t[:, 0:P], half(a, 0), G.ident[:, :])
                    pe.transpose(ps_t[:, P:2 * P], half(a, 1), G.ident[:, :]).then_inc(turned, 1)

                def update(k):
                    def step(t, q, i):
                        pe.wait_ge(winbd_ok, t + 1)
                        pe.wait_ge(ohT_ok, t + 1)
                        if later(t, 1):
                            pe.wait_ge(new_pre[k], t)
                        if k == 0 and known is not None:
                            pe.wait_ge(ea_in[q], 16 * (i + 1))
                        else:
                            pe.wait_ge(featT_ok[k], t + 1)
                        spread = winbd[k][q][:, :, :].rearrange("p j c -> p (j c)")
                        for n in (0, 1):
                            pe.matmul(half(ps_u[k], n), ohT[q][:, :], spread[:, n * P:(n + 1) * P], start=True, stop=False)
                            ins = pe.matmul(half(ps_u[k], n), half(featT[k][q], n), w_edge[k], start=False, stop=True)
                        ins.then_inc(updated[k], 1)
                    return step

                def turn_new(k):
                    def step(t, q, i):
                        if later(t, 1):
                            pe.wait_ge(featT_ok[k + 1], t)
                        pe.wait_ge(new_ok[k], t + 1)
                        a = new[k][q][:, :, :].rearrange("p j c -> p (j c)")
                        pe.transpose(half(ps_n[k], 0), a[:, 0:P], G.ident[:, :])
                        pe.transpose(half(ps_n[k], 1), a[:, P:2 * P], G.ident[:, :]).then_inc(new_turned[k], 1)
                    return step

                def messages(t, q, i):
                    if later(t, 1):
                        pe.wait_ge(msg_pre, t)
                    pe.wait_ge(featT_ok[L], t + 1)
                    pe.matmul(half(ps_m, 0), half(featT[L][q], 0), w_msg, start=True, stop=True)
                    pe.matmul(half(ps_m, 1), half(featT[L][q], 1), w_msg, start=True, stop=True).then_inc(msg_mm, 1)

                def scatter(t, q, i):
                    if L == 0:
                        pe.wait_ge(oh_ok, t + 1)
                    if later(t, 1):
                        pe.wait_ge(added, t)
                    pe.wait_ge(msg_ok, t + 1)
                    for j in range(J):
                        ins = pe.matmul(ps_w[0:D, 0:W], msg[q][:, j, :], oh[q][:, j, :], start=(j == 0), stop=(j == J - 1))
                    ins.then_inc(summed, 1)
                stages = [(turn_at, turn)]
                for k in range(L):
                    stages += [(update_at[k], update(k)), (turn_new_at[k], turn_new(k))]
                pipeline(pe, S.T, halves(stages + [(messages_at, messages), (scatter_at, scatter)]), R)


def node_update_phase(nc, S, G, tag, w_sum, w_self, bias, out):
    with ExitStack() as ctx:
        sb = lambda name, shape, dt: ctx.enter_context(nc.sbuf_tensor(name + tag, shape, dt))
        sem = phase_semaphores(nc, ctx, tag)
        xT = [sb(f"u_xT{u}", [D, P], F32) for u in (0, 1)]
        hid, square = sb("u_hid", [P, S.NB, D], F32), sb("u_square", [P, S.NB, D], F32)
        norm = sb("u_norm", [P, S.NB], F32)
        ps_t = [ctx.enter_context(nc.psum_tensor(f"ps_ut{tag}{u}", [P, 512], F32)) for u in (0, 1)]
        ps_m = [ctx.enter_context(nc.psum_tensor(f"ps_um{tag}{u}", [P, 512], F32)) for u in (0, 1)]
        turned, copied, product, scaled, taken, chain, sq_ok, root_ok = (
            sem("u_" + n) for n in ("turned", "copied", "product", "scaled", "taken", "chain", "sq", "root"))
        with nc.Block() as block:
            @block.tensor
            def _(pe):
                def multiply(b):
                    if b >= 2:
                        pe.wait_ge(taken, b - 1)
                    pe.matmul(ps_m[b % 2][:, 0:D], G.acc[0:D, b * P:(b + 1) * P], w_sum, start=True, stop=True)
                    pe.wait_ge(copied, b + 1)
                    pe.matmul(ps_m[b % 2][:, D:2 * D], xT[b % 2][:, :], w_self, start=True, stop=True).then_inc(product, 1)

                for b in range(S.NB):
                    if b >= 2:
                        pe.wait_ge(copied, b - 1)
                    pe.transpose(ps_t[b % 2][0:D, 0:P], G.x[:, b, :], G.ident[:, :]).then_inc(turned, 1)
                    if b >= 1:
                        multiply(b - 1)
                multiply(S.NB - 1)

            @block.scalar
            def _(act):
                for b in range(S.NB):
                    act.wait_ge(turned, b + 1)
                    if b >= 2:
                        act.wait_ge(product, b - 1)
                    act.copy(xT[b % 2][:, :], ps_t[b % 2][0:D, 0:P]).then_inc(copied, 1)
                act.wait_ge(sq_ok, 1)
                act.activation(norm[:, :], norm[:, :], ACT.Sqrt).then_inc(root_ok, 1)

            @block.vector
            def _(dve):
                for b in range(S.NB):
                    dve.wait_ge(product, b + 1)
                    dve.scalar_tensor_tensor(hid[:, b, :], ps_m[b % 2][:, 0:D], G.inv_cnt[:, b:b + 1], bias, ALU.mult, ALU.add).then_inc(scaled, 1)
                    dve.wait_ge(scaled, b + 1)
                    dve.tensor_tensor(hid[:, b, :], hid[:, b, :], ps_m[b % 2][:, D:2 * D], ALU.add).then_inc(taken, 1)
                dve.wait_ge(taken, S.NB)
                link = Chain(dve, chain)
                link(dve.tensor_scalar(hid[:, :, :], hid[:, :, :], 0.0, None, ALU.max))
                link(dve.tensor_tensor(square[:, :, :], hid[:, :, :], hid[:, :, :], ALU.mult))
                link(dve.reduce_sum(norm[:, :], square[:, :, :], axis=AX.X))
                link(dve.tensor_scalar(norm[:, :], norm[:, :], 1e-24, None, ALU.max))
                dve.sem_inc(sq_ok, 1)
                dve.wait_ge(root_ok, 1)
                link(dve.reciprocal(norm[:, :], norm[:, :]))
                link(dve.tensor_tensor(G.x[:, :, :], hid[:, :, :], norm[:, :].unsqueeze(2).broadcast_to([P, S.NB, D]), ALU.mult))
                if out:
                    link(dve.tensor_tensor(G.y[:, :, :], G.x[:, :, :], G.x0[:, :, :], ALU.add))


def store_phase(nc, S, G, out):
    with ExitStack() as ctx:
        out_done = ctx.enter_context(nc.semaphore("out_done"))
        with nc.Block() as block:
            @block.sync
            def _(sp):
                sp.dma_start(out[0:S.NF * P, :].rearrange("(b p) c -> p b c", p=P), G.x[:, 0:S.NF, :]).then_inc(out_done, 16)
                sp.dma_start(out[S.NF * P:S.N, :], G.x[0:S.NR, S.NF, :]).then_inc(out_done, 16)
                sp.wait_ge(out_done, 32)


class Space:
    pass


def gnn_program(nc, x, src, dst, edge_attr_16, edge_attr_64, W_node, W_edge, attn_src, attn_dst, ln_gamma, ln_beta,
                msg_W, msg_b, agg_W, agg_b, edge_W, edge_b, out):
    S = Shapes(x.shape[0], src.shape[0])
    G = Space()
    C0 = D + H
    dram = lambda name, cols: nc.dram_tensor(name, (S.NP, cols), F32, kind="Internal").ap()
    table0, tableA = dram("table0", C0), dram("table_target", H)
    src_table = [dram(f"src_table{l}", (l + 1) * D) for l in range(3)]
    dst_table = [None] + [dram(f"dst_table{l}", l * D) for l in (1, 2)]
    table_c, target_table_c = dram("table_c", 2 * D), dram("target_table_c", D)
    sparse_table = dram("sparse_table", D)
    features = nc.dram_tensor("features", (S.T * P, J * D), F32, kind="Internal").ap()
    with ExitStack() as ctx:
        sb = lambda name, shape, dt: ctx.enter_context(nc.sbuf_tensor(name, shape, dt))
        G.ident, G.ident_bf = sb("ident", [P, P], F32), sb("ident_bf", [P, P], BF16)
        G.blockmask = sb("blockmask", [P, J, 1], F32)
        G.stack_id = sb("stack_id", [P, W], F32)
        G.iota_w, G.iota_p = sb("iota_w", [P, W], F32), sb("iota_p", [P, P], F16)
        G.ones_bf = sb("ones_bf", [P, 1], BF16)
        G.x, G.y = (sb(n, [P, S.NB, D], F32) for n in ("x", "y"))
        G.src_i, G.dst_i = sb("src_i", [P, S.T * J], I32), sb("dst_i", [P, S.T * J], I32)
        G.real = sb("real", [P, S.T * J], mybir.dt.uint8)
        G.control = sb("control", [1, 4], I32)
        G.inv_cnt = sb("inv_cnt", [P, S.NB], F32)
        G.acc = sb("acc", [C0, S.NP], F32)
        widths = {"w0": D + 2 * H, "w_attn": 2 * H, "w_edge16": J * H, "gamma": D, "beta": D,
                  "table_w0": D, "table_w1": 3 * D, "table_w2": 3 * D, "msg0": P, "msg1": P, "msg2": P, "edge0": P, "edge1": P,
                  "sum0": D, "sum1": D, "sum2": D, "self0": D, "self1": D, "self2": D, "bias0": D, "bias1": D, "bias2": D}
        G.weights = sb("weights", [P, sum(widths.values())], F32)
        at, wt = 0, {}
        for name, width in widths.items():
            wt[name] = G.weights[:, at:at + width]
            at += width
        G.w0, G.w_attn, G.w_edge16, G.gamma, G.beta = (wt[n] for n in ("w0", "w_attn", "w_edge16", "gamma", "beta"))
        flat = lambda a: a.rearrange("(o c) -> o c", o=1)
        everywhere = lambda a: flat(a).broadcast_to([P, D])
        copies = [(G.w0[0:D, 0:D], W_node), (G.gamma, everywhere(ln_gamma)), (G.beta, everywhere(ln_beta))]
        for k, a in enumerate((attn_src, attn_dst)):
            for h in range(H):
                copies.append((G.w_attn[h * HD:(h + 1) * HD, k * H + h:k * H + h + 1], a[h, :].rearrange("(c o) -> c o", o=1)))
        for j in range(J):
            copies.append((G.w_edge16[j * 16:(j + 1) * 16, j * H:(j + 1) * H], W_edge))
        for l in range(3):
            for k in range(2):
                copies.append((wt[f"msg{l}"][k * D:(k + 1) * D, k * D:(k + 1) * D], msg_W[l, D:2 * D, :]))
                if l < 2:
                    copies.append((wt[f"edge{l}"][k * D:(k + 1) * D, k * D:(k + 1) * D], edge_W[l, 2 * D:3 * D, :]))
            copies += [(wt[f"sum{l}"][0:D, :], agg_W[l, 0:D, :]), (wt[f"self{l}"][0:D, :], agg_W[l, D:2 * D, :]),
                       (wt[f"bias{l}"], everywhere(agg_b[l, :]))]
            c = 0 if l == 0 else D
            copies += [(wt[f"table_w{l}"][0:D, c:c + D], msg_W[l, 0:D, :]), (wt[f"table_w{l}"][D:D + 1, c:c + D], flat(msg_b[l, :]))]
            if l:
                copies += [(wt[f"table_w{l}"][0:D, 0:D], edge_W[l - 1, 0:D, :]), (wt[f"table_w{l}"][D:D + 1, 0:D], flat(edge_b[l - 1, :])),
                           (wt[f"table_w{l}"][0:D, 2 * D:3 * D], edge_W[l - 1, D:2 * D, :])]

        G.adj = sb("adj", [P, S.NB, S.NP], mybir.dt.uint8)
        with ExitStack() as edge_ctx:
            esb = lambda name, shape, dt: edge_ctx.enter_context(nc.sbuf_tensor(name, shape, dt))
            G.base_i, G.base_cur = esb("base_i", [1, S.T], I32), esb("base_cur", [1, S.T], I32)
            G.rel, G.window = esb("rel", [P, S.T, J], F32), esb("window", [P, W], F32)
            with ExitStack() as first:
                fsb = lambda name, shape, dt: first.enter_context(nc.sbuf_tensor(name, shape, dt))
                G.iota_key, G.maxima = fsb("iota_key", [P, S.NB * W], F16), fsb("maxima", [H, S.NP], F32)
                G.src_r, G.src_b, G.src_neg = (fsb(n, [P, S.T, J], F32) for n in ("src_r", "src_b", "src_neg"))
                setup_phase(nc, S, G, x, src, dst, copies)
                attention_weights_phase(nc, S, G)
                project_phase(nc, S, G, "0", G.w0[0:D + 1, :], D + 2 * H, [(0, C0, table0), (C0, C0 + H, tableA)])
                passes = nc.values_load(G.control[0:1, 0:1], min_val=1, max_val=S.NW)
                sweeps = nc.values_load(G.control[0:1, 1:2], min_val=1, max_val=2)
                first_window_phase(nc, S, G, "M", [G.maxima[:, :]])
                with nc.Fori(0, sweeps):
                    first_window_phase(nc, S, G, "S", [G.acc[:, :], G.adj[:, :, :]])
                    with nc.Fori(0, passes):
                        attention_phase(nc, S, G, table0, tableA, edge_attr_16)
            attention_nodes_phase(nc, S, G, table0)
            norm_phase(nc, S, G, "0a", True, G.y)
            norm_phase(nc, S, G, "0b", False, G.x)
            with ExitStack() as own:
                propagate(nc, S, G, "1", G.adj, (1.0, 0.8, 0.5, 0.3), G.src_i, G.dst_i, sparse_table,
                          lambda n, s, d: own.enter_context(nc.sbuf_tensor(n, s, d)))
            norm_phase(nc, S, G, "1", False, G.x)
            with nc.sbuf_tensor("x0", [P, S.NB, D], F32) as G.x0:
                keep_x_phase(nc, S, G)
                for l in range(3):
                    outs = [(0, D, src_table[l][:, l * D:(l + 1) * D])]
                    if l:
                        outs = [(0, 2 * D, src_table[l][:, (l - 1) * D:(l + 1) * D]), (2 * D, 3 * D, dst_table[l][:, (l - 1) * D:l * D])]
                    if l == 1:
                        outs += [(0, D, src_table[2][:, 0:D]), (2 * D, 3 * D, dst_table[2][:, 0:D])]
                    else:
                        outs += [(0, 2 * D, table_c), (2 * D, 3 * D, target_table_c)] if l == 2 else []
                    width = 3 * D if l else D
                    project_phase(nc, S, G, "ABC"[l], wt[f"table_w{l}"][0:D + 1, 0:width], width, outs)
                    first_window_phase(nc, S, G, "ABC"[l], [G.acc[:, :]])
                    if l < 2:
                        with nc.Fori(0, passes):
                            edge_phase(nc, S, G, "AB"[l], src_table[l], dst_table[l], [wt["edge0"]][:l], wt[f"msg{l}"], edge_attr_64,
                                       keep=features if l else None)
                    else:
                        with nc.If(passes < 2):
                            nc.all_engine_barrier()
                            edge_phase(nc, S, G, "C", table_c, target_table_c, [wt["edge1"]], wt["msg2"], None,
                                       known=features)
                        nc.end_ifs()
                        nc.all_engine_barrier()
                        with nc.If(passes > 1):
                            nc.all_engine_barrier()
                            with nc.Fori(0, passes):
                                edge_phase(nc, S, G, "Z", src_table[2], dst_table[2], [wt["edge0"], wt["edge1"]], wt["msg2"], edge_attr_64)
                        nc.end_ifs()
                        nc.all_engine_barrier()
                    node_update_phase(nc, S, G, "ABC"[l], wt[f"sum{l}"][0:D, :], wt[f"self{l}"][0:D, :], wt[f"bias{l}"], l == 2)
            norm_phase(nc, S, G, "2", False, G.x)
        with nc.sbuf_tensor("adjT", [P, S.NB, S.NP], mybir.dt.uint8) as adjT:
            transpose_counts_phase(nc, S, G, G.adj, adjT)
            propagate(nc, S, G, "3", adjT, None, G.dst_i, G.src_i, sparse_table, Room(G.adj[:, :, :].rearrange("p b n -> p (b n)")))
        norm_phase(nc, S, G, "3", False, G.x)
        store_phase(nc, S, G, out)


class Room:

    def __init__(self, tile, at=0):
        self.tile, self.at = tile, at

    def __call__(self, name, shape, dt):
        size = shape[1] * (shape[2] if len(shape) > 2 else 1) * (2 if dt == BF16 else 4)
        a = self.tile[:, self.at:self.at + size].bitcast(dt)
        self.at += -(-size // 32) * 32
        return a.rearrange("p (b c) -> p b c", c=shape[2]) if len(shape) > 2 else a

    @property
    def again(self):
        return Room(self.tile, self.at)


def keep_x_phase(nc, S, G):
    with nc.semaphore("kept_x") as done, nc.Block() as block:
        @block.vector
        def _(dve):
            dve.tensor_copy(G.x0[:, :, :], G.x[:, :, :]).then_inc(done, 1)
            dve.wait_ge(done, 1)


_INS = ['x', 'src', 'dst', 'edge_attr_16', 'edge_attr_64', 'L0_gnn_W_node', 'L0_gnn_W_edge', 'L0_gnn_attn_src', 'L0_gnn_attn_dst',
        'L0_gnn_ln_gamma', 'L0_gnn_ln_beta', 'L2_gnn_msg_W', 'L2_gnn_msg_b', 'L2_gnn_agg_W', 'L2_gnn_agg_b', 'L2_gnn_edge_W', 'L2_gnn_edge_b']


def kernel(**inputs):
    import numpy as _np
    import concourse.bacc as _bacc
    from concourse import mybir as _mybir
    from concourse.bass_utils import run_bass_kernel_spmd as _run

    nc = _bacc.Bacc("TRN2", target_bir_lowering=False, num_devices=1)
    arrays, args = {}, []
    for name in _INS:
        a = _np.ascontiguousarray(inputs[name])
        arrays[f"in_{name}_dram"] = a
        args.append(nc.dram_tensor(f"in_{name}_dram", a.shape, _mybir.dt.from_np(a.dtype), kind="ExternalInput").ap())
    args.append(nc.dram_tensor("out_0_dram", inputs["x"].shape, _mybir.dt.float32, kind="ExternalOutput").ap())
    gnn_program(nc, *args)
    r = _run(nc, [arrays], core_ids=[0])
    return r.results[0]["out_0_dram"]
```
